# Optimizing a Trainium2 kernel written in Bass

```python
import numpy as np
import jax
import jax.numpy as jnp

def _softmax(x, axis=-1):
    return jax.nn.softmax(x, axis=axis)

def _gelu(x):
    return jax.nn.gelu(x, approximate=True)

def _silu(x):
    return jax.nn.silu(x)

def _sigmoid(x):
    return jax.nn.sigmoid(x)

def _layernorm(x, axis=-1, eps=1e-05):
    m = jnp.mean(x, axis=axis, keepdims=True)
    v = jnp.var(x, axis=axis, keepdims=True)
    return (x - m) / jnp.sqrt(v + eps)

def _scatter_add(tgt, idx, src, axis=0):
    return tgt.at[idx].add(src)

def _segment_sum(src, seg, n):
    return jax.ops.segment_sum(src, seg, n)
kernel_name = 'mk_cond_resid_d2_seqx_r2_0ec298'

def setup_inputs(seed: int=0):
    np.random.seed(seed)
    _w = jnp.asarray

    def _rec_inputs():
        import jax
        import jax.numpy as jnp
        _rk = jax.random.key(seed)
        x = -7.109e-05 + 0.9999 * jax.random.normal(jax.random.fold_in(_rk, 1), (32, 128, 2048), jnp.float32)
        _lenS = 128 - jax.random.randint(jax.random.fold_in(_rk, 7), (32,), 0, max(1, 128 // 4) + 1, jnp.int32)
        _lenS2 = 128 - jax.random.randint(jax.random.fold_in(_rk, 8), (32,), 0, max(1, 128 // 4) + 1, jnp.int32)
        itok_B_0_15 = jax.random.randint(jax.random.fold_in(_rk, 11), (32,), 0, 16, jnp.int32)
        itok_B_0_7 = jax.random.randint(jax.random.fold_in(_rk, 12), (32,), 0, 8, jnp.int32)
        return (x, itok_B_0_15, itok_B_0_7)
    x, itok_B_0_15, itok_B_0_7 = _rec_inputs()

    def _L0_cond_setup():
        import jax, jax.numpy as jnp
        import numpy as np
        B, C, T = (64, 128, 2048)
        S, D = (16, 128)
        key = jax.random.key(seed)
        k1, k2, k3 = jax.random.split(key, 3)
        x = jax.random.normal(k1, (B, C, T), dtype=jnp.float32)
        condition = jax.random.randint(k2, (B,), 0, S, dtype=jnp.int64)
        bound = float(np.sqrt(6.0 / C))
        weights = jax.random.uniform(k3, (S, C, D), dtype=jnp.float32, minval=-bound, maxval=bound)
        return {'x': x, 'condition': condition, 'weights': weights}
    _L0_cond_all = _L0_cond_setup()
    _L0_cond_in = {k: v for k, v in _L0_cond_all.items() if k in ('weights',)}
    del _L0_cond_all

    def _L1_cond_setup():
        import jax, jax.numpy as jnp
        import numpy as np
        TOP_K = 2
        LANG_BIAS = 5.0
        SCALING = 32.0 / 16.0
        LANGUAGE_PAD_ID = -1
        key = jax.random.key(seed)
        ks = jax.random.split(key, 6)
        B, T, D, O, E, R = (4, 1024, 2048, 2048, 8, 16)
        x = jax.random.normal(ks[0], (B, T, D), dtype=jnp.float32)
        language_ids = jax.random.randint(ks[1], (B,), 0, E).astype(jnp.int64)
        W = jax.random.normal(ks[2], (O, D), dtype=jnp.float32) * (1.0 / np.sqrt(D))
        Wr = jax.random.normal(ks[3], (E, D), dtype=jnp.float32) * (1.0 / np.sqrt(D))
        A = jax.random.normal(ks[4], (E, R, D), dtype=jnp.float32) * (1.0 / np.sqrt(D))
        Bm = jax.random.normal(ks[5], (O, R), dtype=jnp.float32) * 0.0
        Bm = jnp.broadcast_to(Bm, (E, O, R)) + jax.random.normal(ks[5], (E, O, R), dtype=jnp.float32) * 0.02
        return {'x': x, 'language_ids': language_ids, 'W': W, 'Wr': Wr, 'A': A, 'B': Bm}
    _L1_cond_all = _L1_cond_setup()
    _L1_cond_in = {k: v for k, v in _L1_cond_all.items() if k in ('W', 'Wr', 'A', 'B')}
    del _L1_cond_all
    return {'x': x, 'itok_B_0_15': itok_B_0_15, 'itok_B_0_7': itok_B_0_7, 'L0_cond_weights': _L0_cond_in['weights'], 'L1_cond_W': _L1_cond_in['W'], 'L1_cond_Wr': _L1_cond_in['Wr'], 'L1_cond_A': _L1_cond_in['A'], 'L1_cond_B': _L1_cond_in['B']}

def reference(x, itok_B_0_15, itok_B_0_7, L0_cond_weights, L1_cond_W, L1_cond_Wr, L1_cond_A, L1_cond_B):
    import jax
    import jax.numpy as jnp

    def _L0_cond_ref(x, condition, weights):
        import jax, jax.numpy as jnp
        import numpy as np
        B, C, T = (64, 128, 2048)
        S, D = (16, 128)
        W = weights[condition]
        return jnp.einsum('bct,bcd->bdt', x, W)

    def _L1_cond_ref(x, language_ids, W, Wr, A, B):
        import jax, jax.numpy as jnp
        import numpy as np
        TOP_K = 2
        LANG_BIAS = 5.0
        SCALING = 32.0 / 16.0
        LANGUAGE_PAD_ID = -1
        base = jnp.einsum('btd,od->bto', x, W)
        E = Wr.shape[0]
        logits = jnp.einsum('btd,ed->bte', x.astype(jnp.float32), Wr.astype(jnp.float32))
        expert_targets = language_ids
        valid = expert_targets >= 0
        tgt = jnp.where(valid, expert_targets, 0)
        bias = jax.nn.one_hot(tgt, E, dtype=logits.dtype) * LANG_BIAS
        bias = jnp.where(valid[:, None], bias, 0.0)
        logits = logits + bias[:, None, :]
        topw, topi = jax.lax.top_k(logits, TOP_K)
        weights = jax.nn.softmax(topw, axis=-1)
        gates = jnp.sum(jax.nn.one_hot(topi, E, dtype=weights.dtype) * weights[..., None], axis=-2)
        gates = gates.astype(x.dtype)
        h = jnp.einsum('btd,erd->bter', x, A)
        lora_out = jnp.einsum('bter,bte,eor->bto', h, gates, B)
        return base + SCALING * lora_out
    x = x + _L0_cond_ref(x, itok_B_0_15, L0_cond_weights)
    x = x + _L1_cond_ref(x, itok_B_0_7, L1_cond_W, L1_cond_Wr, L1_cond_A, L1_cond_B)
    return x

_drawn_inputs = setup_inputs


def setup_inputs(seed=0):
    import zlib

    import numpy as np

    out = dict(_drawn_inputs(seed))
    spreads = {}
    factors = {}
    for name, (base, spread) in spreads.items():
        noise = np.random.default_rng([zlib.crc32(name.encode()), seed]).standard_normal(out[name].shape)
        drawn = base * np.exp(spread * noise) if base else spread * noise
        out[name] = jnp.asarray(drawn.astype(out[name].dtype))
    for name, factor in factors.items():
        out[name] = (out[name] * factor).astype(out[name].dtype)
    return out
```

```python
from contextlib import ExitStack

import concourse.bass as bass
from concourse import mybir

ALU = mybir.AluOpType
ACT = mybir.ActivationFunctionType
AX = mybir.AxisListType
F32 = mybir.dt.float32
F16 = mybir.dt.float16
I32 = mybir.dt.int32

P = 128
NQ = 512
TOP = 2.0 ** 14
LEAST = 2.0 ** -40
EXPONENT = 0x7F800000
LANG_BIAS = 5.0
SCALING = 2.0
ROUTE_STEPS = 10
W_STEPS = 5
SCALE_STEPS = 5


def cond_resid_kernel(nc, x, cond, lang, w0, wT, wrT, aT, bT, out):
    B, C, D = x.shape
    S = w0.shape[0]
    O = wT.shape[1]
    E = wrT.shape[1]
    ER = aT.shape[1]
    R = ER // E
    K = D // P
    NO = O // NQ
    ND = D // NQ
    RA = ER + E
    PIECE = 4
    NP = K // PIECE
    HALF = 2
    assert C == P and ER == P and D == O and D % NQ == 0 and B % 2 == 0 and E == 8

    with ExitStack() as ctx:
        def sb(name, shape, dt):
            return ctx.enter_context(nc.sbuf_tensor(name, shape, dt))

        def sem(name):
            return ctx.enter_context(nc.semaphore(name))

        w_words = sb("w_words", [P, NO, K, NQ], F32)
        w_parts = w_words[:].bitcast(F16).rearrange("p o k (h n) -> p o k h n", h=2)
        ra_parts = sb("ra_parts", [P, 2, K, RA], F16)
        b_sb = sb("b_sb", [P, O], F32)
        x_in = sb("x_in", [P, 2, D], F32)
        wc = sb("wc", [P, 2, P], F32)
        x1 = sb("x1", [P, 2, D], F32)
        x1_scaled = sb("x1_scaled", [P, D], F32)
        w_scaled = x1_scaled[:].rearrange("p (s k n) -> p s k n", s=2, k=HALF)
        x1t_high = sb("x1t_high", [P, 2, K, P], F16)
        x1t_low = sb("x1t_low", [P, 2, K, P], F16)
        ra_words = x1[:].rearrange("p u d -> p (u d)")[:, 0:K * RA].rearrange("p (k n) -> p k n", k=K)
        ident = sb("ident", [P, P], F32)
        gated = sb("gated", [P, E, R], F32)
        gatedT = sb("gatedT", [P, P], F32)
        ids = sb("ids", [P, 2, B], I32)
        lang_f = sb("lang_f", [P, B], F32)
        expert_no = sb("expert_no", [P, E], F32)
        tie_key = sb("tie_key", [P, E], F32)
        bias = sb("bias", [P, B, E], F32)
        w_max = sb("w_max", [P, NO + 2, NP], F32)
        w_top = sb("w_top", [P, NO + 2], F32)
        w_all = sb("w_all", [P, NO + 2], F32)
        w_pow = sb("w_pow", [P, NO + 2], F32)
        w_inv = sb("w_inv", [P, NO + 2], F32)
        w_scale = sb("w_scale", [P, NO + 2], F32)
        w_back = sb("w_back", [P, NO + 2], F32)
        row = sb("row", [P, 4], F32)
        x_scale = sb("x_scale", [P, 2], F32)
        back = sb("back", [P, 2, NO + 2], F32)
        rt = sb("rt", [P, 6, 8], F32)
        rs = sb("rs", [P, 4], F32)

        sums = [ctx.enter_context(nc.psum_tensor(f"sums{i}", [P, NQ], F32)) for i in range(2)]
        side = [ctx.enter_context(nc.psum_tensor(f"side{i}", [P, NQ], F32)) for i in range(2)]
        turn = [ctx.enter_context(nc.psum_tensor(f"turn{i}", [P, NQ], F32)) for i in range(2)]
        ps_ra = ctx.enter_context(nc.psum_tensor("ps_ra", [P, NQ], F32))
        ps_g = ctx.enter_context(nc.psum_tensor("ps_g", [P, NQ], F32))

        ids_in = sem("ids_in")
        ra_in = sem("ra_in")
        b_in = sem("b_in")
        w_in = [[sem(f"w_in{o}_{p}") for p in range(NP)] for o in range(NO)]
        x_loaded = [sem(f"x_loaded{u}") for u in range(2)]
        stored = [sem(f"stored{u}") for u in range(2)]
        zeroed = sem("zeroed")
        consts_made = sem("consts_made")
        bias_step = sem("bias_step")
        top_found = sem("top_found")
        top_shared = sem("top_shared")
        w_part_max = sem("w_part_max")
        w_step = sem("w_step")
        w_scaled_in = sem("w_scaled_in")
        w_high_in = sem("w_high_in")
        w_low_in = sem("w_low_in")
        ra_high_in = sem("ra_high_in")
        ra_low_in = sem("ra_low_in")
        side_filled = sem("side_filled")
        side_drained = sem("side_drained")
        sums_filled = sem("sums_filled")
        sums_drained = sem("sums_drained")
        scale_step = sem("scale_step")
        x1_scaled_in = sem("x1_scaled_in")
        turned = sem("turned")
        high_in = sem("high_in")
        low_in = sem("low_in")
        ra_filled = sem("ra_filled")
        route_step = sem("route_step")
        exp_in = sem("exp_in")
        gated_in = sem("gated_in")
        gated_turned = sem("gated_turned")
        gatedT_in = sem("gatedT_in")

        block = ctx.enter_context(nc.Block())

        wT_dram = wT.rearrange("(k p) (o n) -> p o k n", p=P, n=NQ)

        @block.sync
        def _(sp):
            def load(b, u):
                sp.dma_start(x_in[:, u, :], x[bass.ds(b, 1), :, :].rearrange("a c t -> (a c) t")
                             ).then_inc(x_loaded[u], 16)
                which = sp.value_load(ids[0:1, 0, bass.ds(b, 1)], min_val=0, max_val=S - 1)
                sp.dma_start(wc[:, u, :], w0[bass.ds(which, 1), :, :].rearrange("a c t -> (a c) t")
                             ).then_inc(x_loaded[u], 16)

            def batch(b, u, loads, ahead):
                if loads:
                    sp.wait_ge(side_drained, b * 8 + 4)
                    load(b + 2, u)
                half = O // 2
                for h in range(2):
                    if h == 0:
                        sp.wait_ge(side_drained, b * 8 + (10 if ahead else 6))
                    else:
                        sp.wait_ge(sums_drained, b * 4 + NO)
                    sp.dma_start(out[bass.ds(b, 1), :, h * half:(h + 1) * half].rearrange("a c t -> (a c) t"),
                                 x1[:, u, h * half:(h + 1) * half]).then_inc(stored[u], 16)

            sp.dma_start(ids[:, 0, :], cond.rearrange("(a b) -> a b", a=1).to_broadcast([P, B])).then_inc(ids_in, 16)
            sp.dma_start(ids[:, 1, :], lang.rearrange("(a b) -> a b", a=1).to_broadcast([P, B])).then_inc(ids_in, 16)
            sp.dma_start(ra_words[:, :, 0:ER], aT.rearrange("(k p) n -> p k n", p=P)).then_inc(ra_in, 16)
            sp.dma_start(ra_words[:, :, ER:RA], wrT.rearrange("(k p) n -> p k n", p=P)).then_inc(ra_in, 16)
            sp.wait_ge(ids_in, 32)
            for b in range(2):
                load(b, b)
            for o in range(NO):
                for p in range(NP):
                    sp.dma_start(w_words[:, o, p * PIECE:(p + 1) * PIECE, :],
                                 wT_dram[:, o, p * PIECE:(p + 1) * PIECE, :]).then_inc(w_in[o][p], 16)
                if o == 0:
                    sp.dma_start(b_sb[:], bT).then_inc(b_in, 16)
            with sp.Fori(0, B // 2 - 1) as pair:
                for u in range(2):
                    batch(pair * 2 + u, u, True, True)
            batch(B - 2, 0, False, True)
            batch(B - 1, 1, False, False)
            for u in range(2):
                sp.wait_ge(stored[u], 16 * B)

        @block.gpsimd
        def _(pool):
            nc.gpsimd.memset(ident[:], 0.0).then_inc(zeroed, 1)
            nc.gpsimd.iota(expert_no[:], [[1, E]], base=0, channel_multiplier=0,
                           allow_small_or_imprecise_dtypes=True).then_inc(consts_made, 1)
            pool.wait_ge(zeroed, 1)
            nc.gpsimd.affine_select(out=ident[:], in_=ident[:], compare_op=ALU.not_equal, fill=1.0, base=0,
                                    pattern=[[-1, P]], channel_multiplier=1).then_inc(consts_made, 1)
            for n in range(NO + 2):
                pool.wait_ge(top_found, n + 1)
                c = (NO + n) if n < 2 else n - 2
                nc.gpsimd.partition_all_reduce(w_all[:, c:c + 1], w_top[:, c:c + 1], P,
                                               bass.bass_isa.ReduceOp.max).then_inc(top_shared, 1)

        @block.tensor
        def _(pe):
            def layer0(b, u, n0):
                pe.wait_ge(x_loaded[u], b * 16 + (32 - 16 * u))
                for j in range(ND):
                    if not (isinstance(n0, int) and n0 + j < 2):
                        pe.wait_ge(side_drained, n0 + (j - 1))
                    nc.tensor.matmul(side[j % 2][:], wc[:, u, :], x_in[:, u, j * NQ:(j + 1) * NQ],
                                     start=True, stop=True).then_inc(side_filled, 1)

            def turn_block(b, u, q):
                if q == 0:
                    pe.wait_ge(x1_scaled_in, b + 1)
                if not (isinstance(b, int) and b == 0 and q < 2):
                    pe.wait_ge(low_in, b * 4 + (q - 1))
                    pe.wait_ge(high_in, b * 4 + (q - 1))
                for j in range(4):
                    k = 4 * q + j
                    mm = nc.tensor.transpose(turn[q % 2][:, j * P:(j + 1) * P],
                                             x1_scaled[:, k * P:(k + 1) * P], ident[:])
                mm.then_inc(turned, 1)

            def products(bank, n, parts, u):
                for k in range(K):
                    for left, part in ((x1t_high, 0), (x1t_high, 1), (x1t_low, 0)):
                        mm = nc.tensor.matmul(bank[:, 0:n], left[:, u, k, :], parts(k, part),
                                              start=(k == 0 and left is x1t_high and part == 0),
                                              stop=(k == K - 1 and left is x1t_low))
                return mm

            def route(b, u):
                pe.wait_ge(high_in, b * 4 + 4)
                pe.wait_ge(low_in, b * 4 + 4)
                if isinstance(b, int) and b == 0:
                    pe.wait_ge(ra_high_in, 2)
                    pe.wait_ge(ra_low_in, 2)
                else:
                    pe.wait_ge(gated_in, b)
                products(ps_ra, RA, lambda k, part: ra_parts[:, part, k, :], u).then_inc(ra_filled, 1)

            def sums_block(b, u, o):
                if isinstance(b, int) and b == 0:
                    pe.wait_ge(w_high_in, (o + 1) * K // HALF)
                    pe.wait_ge(w_low_in, (o + 1) * K // HALF)
                if not (isinstance(b, int) and b == 0 and o < 2):
                    pe.wait_ge(sums_drained, b * 4 + (o - 1))
                products(sums[o % 2], NQ, lambda k, part: w_parts[:, o, k, part, :], u).then_inc(sums_filled, 1)

            def turn_gated(b):
                pe.wait_ge(gated_in, b + 1)
                if not (isinstance(b, int) and b == 0):
                    pe.wait_ge(gatedT_in, b)
                nc.tensor.transpose(ps_g[:, 0:P], gated[:].rearrange("p e r -> p (e r)"), ident[:]
                                    ).then_inc(gated_turned, 1)

            def lora_block(b, j, n):
                if j == 0:
                    pe.wait_ge(gatedT_in, b + 1)
                pe.wait_ge(side_drained, n - 1)
                nc.tensor.matmul(side[j % 2][:], gatedT[:], b_sb[:, j * NQ:(j + 1) * NQ],
                                 start=True, stop=True).then_inc(side_filled, 1)

            def batch(b, u, ahead):
                route(b, u)
                sums_block(b, u, 0)
                if ahead:
                    layer0(b + 1, 1 - u, b * 8 + 4)
                sums_block(b, u, 1)
                turn_gated(b)
                if ahead:
                    turn_block(b + 1, 1 - u, 0)
                    turn_block(b + 1, 1 - u, 1)
                sums_block(b, u, 2)
                lora_base = b * 8 + (8 if ahead else 4)
                for j in range(NO):
                    lora_block(b, j, lora_base + j)
                    if ahead and j % 2 == 0:
                        turn_block(b + 1, 1 - u, 2 + j // 2)
                sums_block(b, u, 3)

            pe.wait_ge(consts_made, 2)
            layer0(0, 0, 0)
            for q in range(4):
                turn_block(0, 0, q)
            pe.wait_ge(b_in, 16)
            for u in range(2):
                batch(u, u, True)
            with pe.Fori(1, B // 2 - 1) as pair:
                for u in range(2):
                    batch(pair * 2 + u, u, True)
            batch(B - 2, 0, True)
            batch(B - 1, 1, False)

        @block.scalar
        def _(act):
            def scale_rows(b, u):
                act.wait_ge(scale_step, b * SCALE_STEPS + SCALE_STEPS)
                if not (isinstance(b, int) and b == 0):
                    act.wait_ge(turned, b * 4)
                else:
                    act.wait_ge(w_low_in, NO * K // HALF)
                nc.scalar.activation(x1_scaled[:], x1[:, u, :], ACT.Copy, scale=x_scale[:, u:u + 1]
                                     ).then_inc(x1_scaled_in, 1)

            def high_part(b, u, q):
                act.wait_ge(turned, b * 4 + (q + 1))
                nc.scalar.activation(x1t_high[:, u, 4 * q:4 * q + 4, :].rearrange("p k n -> p (k n)"),
                                     turn[q % 2][:], ACT.Copy).then_inc(high_in, 1)

            def batch(b, u, ahead):
                act.wait_ge(route_step, b * ROUTE_STEPS + 6)
                nc.scalar.activation(rt[:, 3, :], rt[:, 2, :], ACT.Exp).then_inc(exp_in, 1)
                if ahead:
                    scale_rows(b + 1, 1 - u)
                    high_part(b + 1, 1 - u, 0)
                    high_part(b + 1, 1 - u, 1)
                act.wait_ge(gated_turned, b + 1)
                nc.scalar.activation(gatedT[:], ps_g[:, 0:P], ACT.Copy).then_inc(gatedT_in, 1)
                if ahead:
                    high_part(b + 1, 1 - u, 2)
                    high_part(b + 1, 1 - u, 3)

            for c, cols in enumerate((slice(ER, RA), slice(0, ER))):
                act.wait_ge(w_step, W_STEPS * (c + 1))
                nc.scalar.activation(ra_parts[:, 0, :, cols], ra_words[:, :, cols], ACT.Copy,
                                     scale=w_scale[:, NO + c:NO + c + 1]).then_inc(ra_high_in, 1)
            n = 0
            for o in range(NO):
                act.wait_ge(w_step, W_STEPS * (o + 3))
                for h in range(K // HALF):
                    ks = slice(h * HALF, (h + 1) * HALF)
                    if n >= 2:
                        act.wait_ge(w_low_in, n - 1)
                    nc.scalar.activation(w_scaled[:, n % 2], w_words[:, o, ks, :], ACT.Copy,
                                         scale=w_scale[:, o:o + 1]).then_inc(w_scaled_in, 1)
                    act.wait_ge(w_scaled_in, n + 1)
                    nc.scalar.activation(w_parts[:, o, ks, 0, :], w_scaled[:, n % 2], ACT.Copy).then_inc(w_high_in, 1)
                    n += 1
            scale_rows(0, 0)
            for q in range(4):
                high_part(0, 0, q)
            batch(0, 0, True)
            batch(1, 1, True)
            with act.Fori(1, B // 2 - 1) as pair:
                for u in range(2):
                    batch(pair * 2 + u, u, True)
            batch(B - 2, 0, True)
            batch(B - 1, 1, False)

        @block.vector
        def _(dve):
            def step(ins, which, value):
                ins.then_inc(which, 1)
                dve.wait_ge(which, value)

            def add_layer0(b, u, n0):
                if not (isinstance(b, int) and b < 2):
                    dve.wait_ge(stored[u], b * 16 - 16 * u)
                for j in range(ND):
                    cols = slice(j * NQ, (j + 1) * NQ)
                    dve.wait_ge(side_filled, n0 + (j + 1))
                    nc.vector.tensor_tensor(x1[:, u, cols], side[j % 2][:], x_in[:, u, cols], ALU.add
                                            ).then_inc(side_drained, 1)

            def scale_of_rows(b, u, n0):
                dve.wait_ge(side_drained, n0 + ND)
                s = b * SCALE_STEPS
                step(nc.vector.tensor_reduce(row[:, 0:1], x1[:, u, :], AX.X, ALU.max, apply_absolute_value=True),
                     scale_step, s + 1)
                step(nc.vector.tensor_scalar(row[:, 1:2], row[:, 0:1], LEAST, None, ALU.max), scale_step, s + 2)
                step(nc.vector.tensor_scalar(row[:, 2:3].bitcast(I32), row[:, 1:2].bitcast(I32), EXPONENT, None,
                                             ALU.bitwise_and), scale_step, s + 3)
                nc.vector.tensor_scalar(back[:, u, :], w_back[:], row[:, 2:3], None, ALU.mult)
                step(nc.vector.reciprocal(row[:, 3:4], row[:, 2:3]), scale_step, s + 4)
                nc.vector.tensor_scalar(x_scale[:, u:u + 1], row[:, 3:4], TOP, None, ALU.mult).then_inc(scale_step, 1)

            def low_part(b, u, q):
                dve.wait_ge(high_in, b * 4 + (q + 1))
                nc.vector.tensor_tensor(x1t_low[:, u, 4 * q:4 * q + 4, :].rearrange("p k n -> p (k n)"),
                                        turn[q % 2][:], x1t_high[:, u, 4 * q:4 * q + 4, :].rearrange("p k n -> p (k n)"),
                                        ALU.subtract).then_inc(low_in, 1)

            def gates(b, u):
                dve.wait_ge(ra_filled, b + 1)
                r = b * ROUTE_STEPS
                lg, best, less, ex, key, best_key = (rt[:, i, :] for i in range(6))
                step(nc.vector.scalar_tensor_tensor(lg, ps_ra[:, ER:RA], back[:, u, NO:NO + 1],
                                                    bias[:, bass.ds(b, 1), :].rearrange("p a e -> p (a e)"),
                                                    ALU.mult, ALU.add), route_step, r + 1)
                nc.vector.tensor_scalar(rs[:, 2:3], back[:, u, NO + 1:NO + 2], SCALING, None, ALU.mult
                                        ).then_inc(route_step, 1)
                step(nc.vector.max(best, lg), route_step, r + 3)
                step(nc.vector.scalar_tensor_tensor(key, lg, best[:, 1:2], tie_key[:], ALU.is_equal, ALU.mult),
                     route_step, r + 4)
                step(nc.vector.scalar_tensor_tensor(key, lg, best[:, 1:2], key, ALU.is_gt, ALU.add),
                     route_step, r + 5)
                nc.vector.tensor_scalar(less, lg, best[:, 0:1], None, ALU.subtract).then_inc(route_step, 1)
                step(nc.vector.max(best_key, key), route_step, r + 7)
                dve.wait_ge(exp_in, b + 1)
                step(nc.vector.scalar_tensor_tensor(key, key, best_key[:, 1:2], ex, ALU.is_ge, ALU.mult,
                                                    accum_out=rs[:, 0:1]), route_step, r + 8)
                step(nc.vector.reciprocal(rs[:, 1:2], rs[:, 0:1]), route_step, r + 9)
                step(nc.vector.tensor_scalar(rs[:, 3:4], rs[:, 1:2], rs[:, 2:3], None, ALU.mult), route_step, r + 10)
                if not (isinstance(b, int) and b == 0):
                    dve.wait_ge(gated_turned, b)
                nc.vector.scalar_tensor_tensor(gated[:], ps_ra[:, 0:ER].rearrange("p (e r) -> p e r", e=E),
                                               rs[:, 3:4], key.rearrange("p (e a) -> p e a", a=1).to_broadcast([P, E, R]),
                                               ALU.mult, ALU.mult).then_inc(gated_in, 1)

            def add_sums(b, u, o, lora_base=None):
                cols = slice(o * NQ, (o + 1) * NQ)
                dve.wait_ge(sums_filled, b * 4 + (o + 1))
                if o == 3:
                    dve.wait_ge(side_drained, lora_base + NO)
                nc.vector.scalar_tensor_tensor(x1[:, u, cols], sums[o % 2][:], back[:, u, o:o + 1], x1[:, u, cols],
                                               ALU.mult, ALU.add).then_inc(sums_drained, 1)

            def add_lora(b, u, j, n):
                cols = slice(j * NQ, (j + 1) * NQ)
                dve.wait_ge(side_filled, n + 1)
                if j < 3:
                    dve.wait_ge(sums_drained, b * 4 + (j + 1))
                nc.vector.tensor_tensor(x1[:, u, cols], side[j % 2][:], x1[:, u, cols], ALU.add
                                        ).then_inc(side_drained, 1)

            def batch(b, u, ahead):
                gates(b, u)
                add_sums(b, u, 0)
                if ahead:
                    add_layer0(b + 1, 1 - u, b * 8 + 4)
                    scale_of_rows(b + 1, 1 - u, b * 8 + 4)
                add_sums(b, u, 1)
                if ahead:
                    low_part(b + 1, 1 - u, 0)
                    low_part(b + 1, 1 - u, 1)
                add_sums(b, u, 2)
                base = b * 8 + (8 if ahead else 4)
                for j in range(NO):
                    add_lora(b, u, j, base + j)
                    if ahead and j % 2 == 0:
                        low_part(b + 1, 1 - u, 2 + j // 2)
                add_sums(b, u, 3, base)

            dve.wait_ge(ids_in, 32)
            dve.wait_ge(consts_made, 2)
            step(nc.vector.tensor_copy(lang_f[:], ids[:, 1, :]), bias_step, 1)
            nc.vector.tensor_scalar(tie_key[:], expert_no[:], -1.0 / 16, 0.5, ALU.mult, ALU.add)
            for e in range(E):
                ins = nc.vector.tensor_scalar(bias[:, :, e], lang_f[:], expert_no[:, e:e + 1], LANG_BIAS,
                                              ALU.is_equal, ALU.mult)
            ins.then_inc(bias_step, 1)

            def scale_of_weights(c, n):
                col = slice(c, c + 1)
                s = n * W_STEPS
                dve.wait_ge(top_shared, n + 1)
                step(nc.vector.tensor_scalar(w_all[:, col], w_all[:, col], LEAST, None, ALU.max), w_step, s + 1)
                step(nc.vector.tensor_scalar(w_pow[:, col].bitcast(I32), w_all[:, col].bitcast(I32), EXPONENT, None,
                                             ALU.bitwise_and), w_step, s + 2)
                step(nc.vector.reciprocal(w_inv[:, col], w_pow[:, col]), w_step, s + 3)
                nc.vector.tensor_scalar(w_back[:, col], w_pow[:, col], 1.0 / TOP / TOP, None, ALU.mult
                                        ).then_inc(w_step, 1)
                step(nc.vector.tensor_scalar(w_scale[:, col], w_inv[:, col], TOP, None, ALU.mult), w_step, s + W_STEPS)

            dve.wait_ge(ra_in, 32)
            for c, cols in enumerate((slice(ER, RA), slice(0, ER))):
                nc.vector.tensor_reduce(w_top[:, NO + c:NO + c + 1], ra_words[:, :, cols], AX.XY, ALU.max,
                                        apply_absolute_value=True).then_inc(top_found, 1)
                scale_of_weights(NO + c, c)
                dve.wait_ge(ra_high_in, c + 1)
                nc.vector.scalar_tensor_tensor(ra_parts[:, 1, :, cols], ra_words[:, :, cols],
                                               w_scale[:, NO + c:NO + c + 1], ra_parts[:, 0, :, cols],
                                               ALU.mult, ALU.subtract).then_inc(ra_low_in, 1)
            n = 0
            for o in range(NO):
                for p in range(NP):
                    dve.wait_ge(w_in[o][p], 16)
                    ins = nc.vector.tensor_reduce(w_max[:, o, p:p + 1], w_words[:, o, p * PIECE:(p + 1) * PIECE, :],
                                                  AX.XY, ALU.max, apply_absolute_value=True)
                step(ins, w_part_max, o + 1)
                nc.vector.tensor_reduce(w_top[:, o:o + 1], w_max[:, o, :], AX.X, ALU.max).then_inc(top_found, 1)
                scale_of_weights(o, o + 2)
                for h in range(K // HALF):
                    dve.wait_ge(w_high_in, n + 1)
                    nc.vector.tensor_tensor(w_parts[:, o, h * HALF:(h + 1) * HALF, 1, :], w_scaled[:, n % 2],
                                            w_parts[:, o, h * HALF:(h + 1) * HALF, 0, :], ALU.subtract
                                            ).then_inc(w_low_in, 1)
                    n += 1
            dve.wait_ge(ra_low_in, 2)
            add_layer0(0, 0, 0)
            scale_of_rows(0, 0, 0)
            for q in range(4):
                low_part(0, 0, q)
            batch(0, 0, True)
            batch(1, 1, True)
            with dve.Fori(1, B // 2 - 1) as pair:
                for u in range(2):
                    batch(pair * 2 + u, u, True)
            batch(B - 2, 0, True)
            batch(B - 1, 1, False)


def kernel(x, itok_B_0_15, itok_B_0_7, L0_cond_weights, L1_cond_W, L1_cond_Wr, L1_cond_A, L1_cond_B):
    import numpy as np
    import concourse.bacc as bacc
    from concourse.bass_utils import run_bass_kernel_spmd

    E, R, D = L1_cond_A.shape
    O = L1_cond_W.shape[0]
    arrays = {
        "x": x,
        "cond": itok_B_0_15,
        "lang": itok_B_0_7,
        "w0": L0_cond_weights,
        "wT": np.transpose(L1_cond_W),
        "wrT": np.transpose(L1_cond_Wr),
        "aT": np.transpose(np.reshape(L1_cond_A, (E * R, D))),
        "bT": np.reshape(np.transpose(L1_cond_B, (0, 2, 1)), (E * R, O)),
    }
    arrays = {name: np.ascontiguousarray(a) for name, a in arrays.items()}
    nc = bacc.Bacc("TRN2", target_bir_lowering=False, num_devices=1)
    args = [nc.dram_tensor(name, a.shape, mybir.dt.from_np(a.dtype), kind="ExternalInput").ap()
            for name, a in arrays.items()]
    args.append(nc.dram_tensor("out", x.shape, mybir.dt.float32, kind="ExternalOutput").ap())
    cond_resid_kernel(nc, *args)
    r = run_bass_kernel_spmd(nc, [arrays], core_ids=[0])
    return r.results[0]["out"]
```

```python
from contextlib import ExitStack

import concourse.bass as bass
from concourse import mybir

ALU = mybir.AluOpType
ACT = mybir.ActivationFunctionType
AX = mybir.AxisListType
F32 = mybir.dt.float32
F16 = mybir.dt.float16
I32 = mybir.dt.int32

P = 128
NQ = 512
TOP = 2.0 ** 14
LEAST = 2.0 ** -40
EXPONENT = 0x7F800000
LANG_BIAS = 5.0
SCALING = 2.0
W_STEPS = 5
X_STEPS = 6
RAW_STEPS = 6
TURN_AT = 10
ROUTE_STEPS = 17


def cond_resid_kernel(nc, x, cond, lang, w0, wT, wrT, aT, bT, out):
    B, C, D = x.shape
    S = w0.shape[0]
    O = wT.shape[1]
    E = wrT.shape[1]
    ER = aT.shape[1]
    R = ER // E
    K = D // P
    NO = O // NQ
    RA = ER + E
    GROUP = NQ // P
    NG = K // GROUP
    HALF = 2
    assert C == P and ER == P and D == O and K == 4 * NO and B % 2 == 0 and B >= 6 and E == 8
    WR, A, BT = NO, NO + 1, NO + 2
    NW = NO + 3

    with ExitStack() as ctx:
        def sb(name, shape, dt):
            return ctx.enter_context(nc.sbuf_tensor(name, shape, dt))

        def sem(name):
            return ctx.enter_context(nc.semaphore(name))

        def bank(name):
            return ctx.enter_context(nc.psum_tensor(name, [P, NQ], F32))

        w_words = sb("w_words", [P, NO, K, NQ], F32)
        w_parts = w_words[:].bitcast(F16).rearrange("p o k (h n) -> p o k h n", h=2)
        ra_parts = sb("ra_parts", [P, K, 2, RA], F16)
        wr_words = sb("wr_words", [P, K, E], F32)
        b_parts = sb("b_parts", [P, NO, 2, NQ], F16)
        x_in = sb("x_in", [P, D], F32)
        wc_in = sb("wc_in", [P, P], F32)
        wc = sb("wc", [P, P], F32)
        x_parts = sb("x_parts", [P, 2, D], F16)
        wc_parts = sb("wc_parts", [P, 2, P], F16)
        x1_raw = sb("x1_raw", [P, D], F32)
        x1_parts = sb("x1_parts", [P, 2, 2, K, P], F16)
        out_sb = sb("out_sb", [P, 2, D], F32)
        ident = sb("ident", [P, P], F32)
        chosen = sb("chosen", [P, E, R], F32)
        gated = sb("gated", [P, P], F32)
        gated_parts = sb("gated_parts", [P, 2, P], F16)
        ids = sb("ids", [P, 2, B], I32)
        lang_f = sb("lang_f", [P, B], F32)
        expert_no = sb("expert_no", [P, E], F32)
        tie_key = sb("tie_key", [P, E], F32)
        bias = sb("bias", [P, B, E], F32)
        w_max = sb("w_max", [P, NO, K // GROUP], F32)
        w_top = sb("w_top", [P, NW], F32)
        w_all = sb("w_all", [P, NW], F32)
        w_pow = sb("w_pow", [P, NW], F32)
        w_inv = sb("w_inv", [P, NW], F32)
        w_scale = sb("w_scale", [P, NW], F32)
        w_back = sb("w_back", [P, NW], F32)
        x_top = sb("x_top", [P, 2], F32)
        x_all = sb("x_all", [P, 2], F32)
        x_pow = sb("x_pow", [P, 2], F32)
        x_scale = sb("x_scale", [P, 2], F32)
        raw_top = sb("raw_top", [P, 1], F32)
        raw_all = sb("raw_all", [P, 1], F32)
        raw_pow = sb("raw_pow", [P, 1], F32)
        raw_scale = sb("raw_scale", [P, 1], F32)
        x_back = sb("x_back", [P, 3], F32)
        pair_back = sb("pair_back", [P, 2, NO], F32)
        back = sb("back", [P, 2, NW], F32)
        rt = sb("rt", [P, 6, E], F32)
        rs = sb("rs", [P, 8], F32)
        lora_back = sb("lora_back", [P, 2], F32)
        pool_scratch = sb("pool_scratch", [P, 1], F32)

        sums = [bank(f"sums{i}") for i in range(2)]
        lora = [bank(f"lora{i}") for i in range(2)]
        raw = [bank(f"raw{i}") for i in range(2)]
        ps_ra = bank("ps_ra")
        ps_g = bank("ps_g")

        w_at = [w_words[:, NO - 1 if o == 0 else o] for o in range(NO)]
        a_words = x1_parts[:, 1].rearrange("p h k n -> p (h k n)").bitcast(F32).rearrange("p (k n) -> p k n", n=ER)
        b_words = out_sb[:, 0, :].rearrange("p (o n) -> p o n", n=NQ)

        pieces = [(a_words, ra_parts[:, :, 0, 0:ER], ra_parts[:, :, 1, 0:ER], A, None),
                  (wr_words[:], ra_parts[:, :, 0, ER:RA], ra_parts[:, :, 1, ER:RA], WR, None)]
        ra_done = len(pieces)
        first_w = []
        for o in range(NO):
            first_w.append(len(pieces))
            for h in range(K // HALF):
                ks = slice(h * HALF, (h + 1) * HALF)
                spot = x1_raw[:, (h % 2) * HALF * NQ:(h % 2 + 1) * HALF * NQ].rearrange("p (k n) -> p k n", n=NQ)
                pieces.append((w_at[o][:, ks, :], w_parts[:, o, ks, 0, :], w_parts[:, o, ks, 1, :], o,
                               None if o == 0 else spot))
            if o == 0:
                first_b = len(pieces)
                pieces.append((b_words, b_parts[:, :, 0, :], b_parts[:, :, 1, :], BT, None))
                b_done = len(pieces)
        in_place = first_w[1]
        per_w = K // HALF
        w_done = [first_w[o] + per_w for o in range(NO)]
        order = [A, WR, 0, BT] + list(range(1, NO))
        turn_of = {c: n for n, c in enumerate(order)}
        ON_ACT = (2, 3)

        ids_in = sem("ids_in")
        a_in = sem("a_in")
        wr_in = sem("wr_in")
        b_in = sem("b_in")
        w_in = [[sem(f"w_in{o}_{g}") for g in range(NG)] for o in range(NO)]
        x_loaded = sem("x_loaded")
        stored = [sem(f"stored{u}") for u in range(2)]
        zeroed = sem("zeroed")
        consts_made = sem("consts_made")
        diagonal_in = sem("diagonal_in")
        bias_step = sem("bias_step")
        w_bound_in = sem("w_bound_in")
        w_part_max = sem("w_part_max")
        top_found = sem("top_found")
        top_shared = sem("top_shared")
        w_step = sem("w_step")
        scaled_in = sem("scaled_in")
        w_high_in = sem("w_high_in")
        w_low_in = sem("w_low_in")
        x_top_found = sem("x_top_found")
        x_top_shared = sem("x_top_shared")
        x_step = sem("x_step")
        x_high_in = sem("x_high_in")
        x_low_in = sem("x_low_in")
        raw_filled = sem("raw_filled")
        raw_drained = sem("raw_drained")
        raw_top_found = sem("raw_top_found")
        raw_top_shared = sem("raw_top_shared")
        raw_step = sem("raw_step")
        x1_high_in = sem("x1_high_in")
        x1_low_in = sem("x1_low_in")
        pair_back_in = sem("pair_back_in")
        ra_filled = sem("ra_filled")
        route_step = sem("route_step")
        exp_in = sem("exp_in")
        gated_in = sem("gated_in")
        gated_turned = sem("gated_turned")
        gated_high_in = sem("gated_high_in")
        gated_low_in = sem("gated_low_in")
        lora_filled = sem("lora_filled")
        lora_drained = sem("lora_drained")
        sums_filled = sem("sums_filled")
        sums_drained = sem("sums_drained")

        block = ctx.enter_context(nc.Block())

        wT_dram = wT.rearrange("(k p) (o n) -> p o k n", p=P, n=NQ)
        LAST = NO - 1
        LOOP = (2, B // 2 - 1)

        def known(b, below):
            return isinstance(b, int) and b < below

        @block.sync
        def _(sp):
            def load(b):
                if not known(b, 1):
                    sp.wait_ge(x_low_in, b * 2)
                sp.dma_start(x_in[:], x[bass.ds(b, 1), :, :].rearrange("a c t -> (a c) t")
                             ).then_inc(x_loaded, 16)
                which = sp.value_load(ids[0:1, 0, bass.ds(b, 1)], min_val=0, max_val=S - 1)
                sp.dma_start(wc_in[:], w0[bass.ds(which, 1), :, :].rearrange("a c t -> (a c) t")
                             ).then_inc(x_loaded, 16)

            def store(b, u, cols, m):
                sp.wait_ge(sums_drained, m)
                sp.dma_start(out[bass.ds(b, 1), :, cols].rearrange("a c t -> (a c) t"),
                             out_sb[:, u, cols]).then_inc(stored[u], 16)

            def load_w(o):
                for g in range(NG):
                    ks = slice(g * GROUP, (g + 1) * GROUP)
                    sp.dma_start(w_at[o][:, ks, :], wT_dram[:, o, ks, :]).then_inc(w_in[o][g], 16)

            front, back_cols = slice(0, LAST * NQ), slice(LAST * NQ, O)
            sp.dma_start(ids[:, 0, :], cond.rearrange("(a b) -> a b", a=1).to_broadcast([P, B])).then_inc(ids_in, 16)
            sp.dma_start(ids[:, 1, :], lang.rearrange("(a b) -> a b", a=1).to_broadcast([P, B])).then_inc(ids_in, 16)
            sp.wait_ge(ids_in, 32)
            load(0)
            sp.dma_start(a_words, aT.rearrange("(k p) n -> p k n", p=P)).then_inc(a_in, 16)
            sp.dma_start(wr_words[:], wrT.rearrange("(k p) n -> p k n", p=P)).then_inc(wr_in, 16)
            load_w(0)
            load(1)
            sp.dma_start(out_sb[:, 0, :], bT).then_inc(b_in, 16)
            for o in range(1, NO):
                if o == NO - 1:
                    sp.wait_ge(w_low_in, w_done[0])
                load_w(o)
            load(2)
            for u in range(2):
                store(u, u, front, 2 * LAST)
            for u in range(2):
                store(u, u, back_cols, 2 * LAST + u + 1)

            def batch(b, u, loads):
                if loads:
                    load(b + 1)
                store(b, u, front, b * NO + LAST)
                store(b, u, back_cols, b * NO + NO)

            batch(2, 0, True)
            batch(3, 1, True)
            with sp.Fori(*LOOP) as pair:
                for u in range(2):
                    batch(pair * 2 + u, u, True)
            batch(B - 2, 0, True)
            batch(B - 1, 1, False)
            for u in range(2):
                sp.wait_ge(stored[u], 16 * B)

        @block.gpsimd
        def _(pool):
            def share(found, value, all_, top, shared):
                pool.wait_ge(found, value)
                nc.gpsimd.tensor_tensor(pool_scratch[:], expert_no[:, 0:1], expert_no[:, 0:1], ALU.add)
                nc.gpsimd.partition_all_reduce(all_, top, P, bass.bass_isa.ReduceOp.max).then_inc(shared, 1)

            def share_w(c, after=None):
                if after is not None:
                    pool.wait_ge(*after)
                col = slice(c, c + 1)
                share(top_found, turn_of[c] + 1, w_all[:, col], w_top[:, col], top_shared)

            def share_x(b):
                share(x_top_found, b + 1, x_all[:], x_top[:], x_top_shared)

            def share_raw(b):
                share(raw_top_found, b + 1, raw_all[:], raw_top[:], raw_top_shared)

            def add_diagonal(o):
                pool.wait_ge(w_in[o][o], 16)
                for g in range(GROUP):
                    spot = w_at[o][:, o * GROUP + g, g * P:(g + 1) * P]
                    ins = nc.gpsimd.tensor_tensor(spot, spot, ident[:], ALU.add)
                ins.then_inc(diagonal_in, 1)

            nc.gpsimd.memset(ident[:], 0.0).then_inc(zeroed, 1)
            nc.gpsimd.iota(expert_no[:], [[1, E]], base=0, channel_multiplier=0,
                           allow_small_or_imprecise_dtypes=True).then_inc(consts_made, 1)
            pool.wait_ge(zeroed, 1)
            nc.gpsimd.affine_select(out=ident[:], in_=ident[:], compare_op=ALU.not_equal, fill=1.0, base=0,
                                    pattern=[[-1, P]], channel_multiplier=1).then_inc(consts_made, 1)
            pool.wait_ge(consts_made, 2)
            share_x(0)
            share_w(A, (x_top_shared, 1))
            share_w(WR, (top_shared, 1))
            add_diagonal(0)
            share_raw(0)
            share_w(0)
            share_w(BT, (top_shared, turn_of[BT]))
            share_x(1)
            share_raw(1)
            for o in range(1, NO):
                add_diagonal(o)
                if o == NO - 1:
                    share_x(2)
                share_w(o)
            share_raw(2)
            share_x(3)
            share_raw(3)
            share_x(4)
            share_raw(4)
            with pool.Fori(*LOOP) as pair:
                for u in range(2):
                    share_x(pair * 2 + (u + 1))
                    share_raw(pair * 2 + (u + 1))
            share_x(B - 1)
            share_raw(B - 1)

        @block.tensor
        def _(pe):
            def layer0(b):
                pe.wait_ge(x_low_in, b * 2 + 2)
                for g in range(NG):
                    if not known(b * NG + g, 2):
                        pe.wait_ge(raw_drained, b * NG + (g - 1))
                    for j in range(GROUP):
                        k = g * GROUP + j
                        for left, right in ((0, 0), (0, 1), (1, 0)):
                            mm = nc.tensor.matmul(raw[g % 2][:, j * P:(j + 1) * P],
                                                  x_parts[:, left, k * P:(k + 1) * P], wc_parts[:, right, :],
                                                  start=(left + right == 0), stop=(left == 1))
                    mm.then_inc(raw_filled, 1)

            def products(bank, n, parts, u, ks=range(K)):
                for k in ks:
                    for left, right in ((0, 0), (0, 1), (1, 0)):
                        mm = nc.tensor.matmul(bank[:, 0:n], x1_parts[:, u, left, k, :], parts(k, right),
                                              start=(k == 0 and left + right == 0),
                                              stop=(k == K - 1 and left == 1))
                return mm

            def route(b, u):
                pe.wait_ge(x1_low_in, b + 1)
                if known(b, 1):
                    pe.wait_ge(w_low_in, ra_done)
                else:
                    pe.wait_ge(route_step, b * ROUTE_STEPS)
                products(ps_ra, RA, lambda k, part: ra_parts[:, k, part, :], u).then_inc(ra_filled, 1)

            def sums_block(u, o, m, gated_of=None):
                if known(m, 2 * NO):
                    pe.wait_ge(w_low_in, w_done[o])
                if not known(m, 2):
                    pe.wait_ge(sums_drained, m - 1)
                bank = sums[(m if isinstance(m, int) else o) % 2]
                parts = lambda k, part: w_parts[:, o, k, part, :]
                if gated_of is None:
                    products(bank, NQ, parts, u).then_inc(sums_filled, 1)
                else:
                    products(bank, NQ, parts, u, range(TURN_AT))
                    turn_gated(gated_of)
                    products(bank, NQ, parts, u, range(TURN_AT, K)).then_inc(sums_filled, 1)

            def turn_gated(b):
                pe.wait_ge(gated_in, b + 1)
                if not known(b, 1):
                    pe.wait_ge(gated_low_in, b)
                nc.tensor.transpose(ps_g[:, 0:P], gated[:], ident[:]).then_inc(gated_turned, 1)

            def lora_product(b):
                pe.wait_ge(gated_high_in, b + 1)
                pe.wait_ge(gated_low_in, b + 1)
                if known(b, 1):
                    pe.wait_ge(w_low_in, b_done)
                for j in range(NO):
                    if not known(b * NO + j, 2):
                        pe.wait_ge(lora_drained, b * NO + (j - 1))
                    for left, right in ((0, 0), (0, 1), (1, 0)):
                        mm = nc.tensor.matmul(lora[j % 2][:], gated_parts[:, left, :], b_parts[:, j, right, :],
                                              start=(left + right == 0), stop=(left == 1))
                    mm.then_inc(lora_filled, 1)

            def batch(b, u, ahead):
                route(b, u)
                sums_block(u, 0, b * NO, gated_of=b)
                lora_product(b)
                sums_block(u, 1, b * NO + 1)
                if ahead:
                    layer0(b + 1)
                sums_block(u, 2, b * NO + 2)
                sums_block(u, 3, b * NO + 3)

            layer0(0)
            for u in range(2):
                route(u, u)
                sums_block(u, 0, u, gated_of=u)
                if u == 0:
                    layer0(1)
                lora_product(u)
            for o in range(1, LAST):
                for u in range(2):
                    sums_block(u, o, 2 * o + u)
            layer0(2)
            for u in range(2):
                sums_block(u, LAST, 2 * LAST + u)
            batch(2, 0, True)
            batch(3, 1, True)
            with pe.Fori(*LOOP) as pair:
                for u in range(2):
                    batch(pair * 2 + u, u, True)
            batch(B - 2, 0, True)
            batch(B - 1, 1, False)

        @block.scalar
        def _(act):
            def split_piece(n):
                words, high, low, c, spot = pieces[n]
                scale = w_scale[:, c:c + 1]
                act.wait_ge(w_step, W_STEPS * turn_of[c] + W_STEPS)
                if spot is None:
                    nc.scalar.activation(high, words, ACT.Copy, scale=scale).then_inc(w_high_in, 1)
                    return
                act.wait_ge(w_low_in, n - 1)
                if n == in_place:
                    act.wait_ge(x1_low_in, 2)
                nc.scalar.activation(spot, words, ACT.Copy, scale=scale).then_inc(scaled_in, 1)
                act.wait_ge(scaled_in, n - in_place + 1)
                nc.scalar.activation(high, spot, ACT.Copy).then_inc(w_high_in, 1)

            def bound_w(g):
                act.wait_ge(w_in[0][g], 16)
                if g != ON_ACT[0]:
                    act.wait_ge(w_bound_in, 1)
                nc.scalar.activation(out_sb[:, 1, :].rearrange("p (k n) -> p k n", n=NQ),
                                     w_at[0][:, g * GROUP:(g + 1) * GROUP, :], ACT.Abs,
                                     accum_out=w_max[:, 0, g:g + 1]).then_inc(w_bound_in, 1)

            def split_x(b):
                act.wait_ge(x_step, b * X_STEPS + 5)
                if not known(b, 1):
                    act.wait_ge(raw_filled, b * NG)
                nc.scalar.activation(x_parts[:, 0, :], x_in[:], ACT.Copy, scale=x_scale[:, 0:1]
                                     ).then_inc(x_high_in, 1)

            def copy_raw(b):
                if known(b, 3) and b == 2:
                    act.wait_ge(w_low_in, len(pieces))
                if not known(b, 1):
                    act.wait_ge(x1_low_in, b)
                for g in range(NG):
                    act.wait_ge(raw_filled, b * NG + (g + 1))
                    nc.scalar.activation(x1_raw[:, g * NQ:(g + 1) * NQ], raw[g % 2][:], ACT.Copy
                                         ).then_inc(raw_drained, 1)

            def split_x1(b, u):
                act.wait_ge(raw_step, b * RAW_STEPS + RAW_STEPS)
                if known(b, 2):
                    act.wait_ge(w_low_in, ra_done)
                else:
                    act.wait_ge(sums_filled, 2 * LAST + 1 if known(b, 3) else (b - 1) * NO)
                nc.scalar.activation(x1_parts[:, u, 0, :, :].rearrange("p k n -> p (k n)"), x1_raw[:], ACT.Copy,
                                     scale=raw_scale[:, 0:1]).then_inc(x1_high_in, 1)

            def exponentials(b):
                act.wait_ge(route_step, b * ROUTE_STEPS + 6)
                nc.scalar.activation(rt[:, 3, :], rt[:, 2, :], ACT.Exp).then_inc(exp_in, 1)

            def split_gated(b):
                act.wait_ge(gated_turned, b + 1)
                nc.scalar.activation(gated_parts[:, 0, :], ps_g[:, 0:P], ACT.Copy).then_inc(gated_high_in, 1)

            def copy_lora(b, u):
                act.wait_ge(route_step, b * ROUTE_STEPS + ROUTE_STEPS)
                if known(b, 2):
                    act.wait_ge(w_low_in, b_done)
                else:
                    act.wait_ge(stored[u], b * 16 - 16 * u)
                for j in range(NO):
                    act.wait_ge(lora_filled, b * NO + (j + 1))
                    nc.scalar.activation(out_sb[:, u, j * NQ:(j + 1) * NQ], lora[j % 2][:], ACT.Copy,
                                         scale=lora_back[:, u:u + 1]).then_inc(lora_drained, 1)

            def split_pieces(first, count):
                for n in range(first, first + count):
                    split_piece(n)

            def batch(b, u, ahead):
                exponentials(b)
                split_gated(b)
                if ahead:
                    split_x(b + 1)
                copy_lora(b, u)
                if ahead:
                    copy_raw(b + 1)
                    split_x1(b + 1, 1 - u)

            split_x(0)
            split_pieces(0, ra_done)
            copy_raw(0)
            for g in ON_ACT:
                bound_w(g)
            split_x1(0, 0)
            split_pieces(first_w[0], per_w)
            exponentials(0)
            split_gated(0)
            split_x(1)
            split_pieces(first_b, b_done - first_b)
            copy_raw(1)
            copy_lora(0, 0)
            split_x1(1, 1)
            exponentials(1)
            split_gated(1)
            split_pieces(first_w[1], 4)
            copy_lora(1, 1)
            split_pieces(first_w[1] + 4, per_w - 4)
            split_pieces(first_w[2], per_w)
            split_x(2)
            split_pieces(first_w[3], per_w)
            copy_raw(2)
            split_x1(2, 0)
            batch(2, 0, True)
            batch(3, 1, True)
            with act.Fori(*LOOP) as pair:
                for u in range(2):
                    batch(pair * 2 + u, u, True)
            batch(B - 2, 0, True)
            batch(B - 1, 1, False)

        @block.vector
        def _(dve):
            def step(ins, which, value):
                ins.then_inc(which, 1)
                dve.wait_ge(which, value)

            def power_and_inverse(which, s, all_, pow_, inv):
                step(nc.vector.tensor_scalar(all_, all_, LEAST, None, ALU.max), which, s + 1)
                step(nc.vector.tensor_scalar(pow_.bitcast(I32), all_.bitcast(I32), EXPONENT, None,
                                             ALU.bitwise_and), which, s + 2)
                step(nc.vector.reciprocal(inv, pow_), which, s + 3)

            def find_part(o, g):
                dve.wait_ge(w_in[o][g], 16)
                if g == o:
                    dve.wait_ge(diagonal_in, o + 1)
                nc.vector.tensor_reduce(w_max[:, o, g:g + 1], w_at[o][:, g * GROUP:(g + 1) * GROUP, :],
                                        AX.XY, ALU.max, apply_absolute_value=True).then_inc(w_part_max, 1)

            def join_parts(o, found):
                dve.wait_ge(w_part_max, found)
                if o == 0:
                    dve.wait_ge(w_bound_in, len(ON_ACT))
                nc.vector.tensor_reduce(w_top[:, o:o + 1], w_max[:, o, :], AX.X, ALU.max).then_inc(top_found, 1)

            def find_top(c):
                arrived, words = {A: (a_in, a_words), WR: (wr_in, wr_words[:]), BT: (b_in, b_words)}[c]
                dve.wait_ge(arrived, 16)
                nc.vector.tensor_reduce(w_top[:, c:c + 1], words, AX.XY, ALU.max, apply_absolute_value=True
                                        ).then_inc(top_found, 1)

            def scale_w(c):
                col = slice(c, c + 1)
                s = turn_of[c] * W_STEPS
                dve.wait_ge(top_shared, turn_of[c] + 1)
                power_and_inverse(w_step, s, w_all[:, col], w_pow[:, col], w_inv[:, col])
                nc.vector.tensor_scalar(w_back[:, col], w_pow[:, col], 1.0 / TOP, None, ALU.mult).then_inc(w_step, 1)
                nc.vector.tensor_scalar(w_scale[:, col], w_inv[:, col], TOP, None, ALU.mult).then_inc(w_step, 1)

            def split_pieces(first, count):
                for n in range(first, first + count):
                    words, high, low, c, spot = pieces[n]
                    dve.wait_ge(w_high_in, n + 1)
                    if spot is None:
                        nc.vector.scalar_tensor_tensor(low, words, w_scale[:, c:c + 1], high, ALU.mult, ALU.subtract
                                                       ).then_inc(w_low_in, 1)
                    else:
                        nc.vector.tensor_tensor(low, spot, high, ALU.subtract).then_inc(w_low_in, 1)

            def find_x_top(b):
                dve.wait_ge(x_loaded, b * 32 + 32)
                if not known(b, 1):
                    dve.wait_ge(x_low_in, b * 2)
                s = b * X_STEPS
                nc.vector.tensor_tensor(wc[:], wc_in[:], ident[:], ALU.add).then_inc(x_step, 1)
                nc.vector.tensor_reduce(x_top[:, 0:1], x_in[:], AX.X, ALU.max, apply_absolute_value=True)
                dve.wait_ge(x_step, s + 1)
                nc.vector.tensor_reduce(x_top[:, 1:2], wc[:], AX.X, ALU.max, apply_absolute_value=True
                                        ).then_inc(x_top_found, 1)

            def split_x(b):
                s = b * X_STEPS
                dve.wait_ge(x_top_shared, b + 1)
                power_and_inverse(x_step, s + 1, x_all[:], x_pow[:], x_scale[:])
                step(nc.vector.tensor_scalar(x_scale[:], x_scale[:], TOP, None, ALU.mult), x_step, s + 5)
                nc.vector.tensor_scalar(x_back[:, 0:1], x_pow[:, 0:1], x_pow[:, 1:2], TOP ** -3, ALU.mult, ALU.mult)
                if not known(b, 1):
                    dve.wait_ge(raw_filled, b * NG)
                step(nc.vector.tensor_scalar(wc_parts[:, 0, :], wc[:], x_scale[:, 1:2], None, ALU.mult),
                     x_step, s + 6)
                nc.vector.scalar_tensor_tensor(wc_parts[:, 1, :], wc[:], x_scale[:, 1:2], wc_parts[:, 0, :],
                                               ALU.mult, ALU.subtract).then_inc(x_low_in, 1)
                dve.wait_ge(x_high_in, b + 1)
                nc.vector.scalar_tensor_tensor(x_parts[:, 1, :], x_in[:], x_scale[:, 0:1], x_parts[:, 0, :],
                                               ALU.mult, ALU.subtract).then_inc(x_low_in, 1)

            def find_raw_top(b):
                dve.wait_ge(raw_drained, b * NG + NG)
                nc.vector.tensor_reduce(raw_top[:], x1_raw[:], AX.X, ALU.max, apply_absolute_value=True
                                        ).then_inc(raw_top_found, 1)

            def split_x1(b, u):
                s = b * RAW_STEPS
                dve.wait_ge(raw_top_shared, b + 1)
                power_and_inverse(raw_step, s, raw_all[:], raw_pow[:], raw_scale[:])
                powers = x_back[:, 1 + u:2 + u]
                step(nc.vector.tensor_scalar(powers, raw_pow[:], x_back[:, 0:1], None, ALU.mult), raw_step, s + 4)
                cols = slice(WR, A + 1) if known(b, 2) else slice(0, NW)
                nc.vector.tensor_scalar(back[:, u, cols], w_back[:, cols], powers, None, ALU.mult
                                        ).then_inc(raw_step, 1)
                step(nc.vector.tensor_scalar(raw_scale[:], raw_scale[:], TOP, None, ALU.mult), raw_step, s + 6)
                dve.wait_ge(x1_high_in, b + 1)
                nc.vector.scalar_tensor_tensor(x1_parts[:, u, 1, :, :].rearrange("p k n -> p (k n)"), x1_raw[:],
                                               raw_scale[:, 0:1],
                                               x1_parts[:, u, 0, :, :].rearrange("p k n -> p (k n)"),
                                               ALU.mult, ALU.subtract).then_inc(x1_low_in, 1)

            def gates(b, u):
                dve.wait_ge(ra_filled, b + 1)
                r = b * ROUTE_STEPS
                lg, best, less, ex, key, best_key = (rt[:, i, :] for i in range(6))
                total, inv_total, factor, weight, row_top, row_pow, row_inv, row_scale = (
                    rs[:, i:i + 1] for i in range(8))
                step(nc.vector.scalar_tensor_tensor(lg, ps_ra[:, ER:RA], back[:, u, WR:WR + 1],
                                                    bias[:, bass.ds(b, 1), :].rearrange("p a e -> p (a e)"),
                                                    ALU.mult, ALU.add), route_step, r + 1)
                nc.vector.tensor_scalar(factor, back[:, u, A:A + 1], SCALING / TOP, None, ALU.mult
                                        ).then_inc(route_step, 1)
                step(nc.vector.max(best, lg), route_step, r + 3)
                step(nc.vector.scalar_tensor_tensor(key, lg, best[:, 1:2], tie_key[:], ALU.is_equal, ALU.mult),
                     route_step, r + 4)
                step(nc.vector.scalar_tensor_tensor(key, lg, best[:, 1:2], key, ALU.is_gt, ALU.add),
                     route_step, r + 5)
                nc.vector.tensor_scalar(less, lg, best[:, 0:1], None, ALU.subtract).then_inc(route_step, 1)
                step(nc.vector.max(best_key, key), route_step, r + 7)
                dve.wait_ge(exp_in, b + 1)
                step(nc.vector.scalar_tensor_tensor(key, key, best_key[:, 1:2], ex, ALU.is_ge, ALU.mult,
                                                    accum_out=total), route_step, r + 8)
                step(nc.vector.reciprocal(inv_total, total), route_step, r + 9)
                step(nc.vector.tensor_scalar(weight, inv_total, factor, None, ALU.mult), route_step, r + 10)
                step(nc.vector.tensor_tensor(chosen[:], ps_ra[:, 0:ER].rearrange("p (e r) -> p e r", e=E),
                                             key.rearrange("p (e a) -> p e a", a=1).to_broadcast([P, E, R]),
                                             ALU.mult), route_step, r + 11)
                step(nc.vector.tensor_reduce(row_top, chosen[:], AX.XY, ALU.max, apply_absolute_value=True),
                     route_step, r + 12)
                power_and_inverse(route_step, r + 12, row_top, row_pow, row_inv)
                nc.vector.tensor_scalar(lora_back[:, u:u + 1], row_pow, weight, w_back[:, BT:BT + 1],
                                        ALU.mult, ALU.mult).then_inc(route_step, 1)
                step(nc.vector.tensor_scalar(row_scale, row_inv, TOP, None, ALU.mult), route_step, r + 17)
                if not known(b, 1):
                    dve.wait_ge(gated_turned, b)
                nc.vector.tensor_scalar(gated[:], chosen[:].rearrange("p e r -> p (e r)"), row_scale, None, ALU.mult
                                        ).then_inc(gated_in, 1)

            def split_gated(b):
                dve.wait_ge(gated_high_in, b + 1)
                if not known(b, 1):
                    dve.wait_ge(lora_filled, b * NO)
                nc.vector.tensor_tensor(gated_parts[:, 1, :], ps_g[:, 0:P], gated_parts[:, 0, :], ALU.subtract
                                        ).then_inc(gated_low_in, 1)

            def powers_of_pair(o):
                dve.wait_ge(w_step, W_STEPS * turn_of[o] + W_STEPS)
                dve.wait_ge(raw_step, 2 * RAW_STEPS)
                for u in range(2):
                    nc.vector.tensor_scalar(pair_back[:, u, o:o + 1], w_back[:, o:o + 1], x_back[:, 1 + u:2 + u], None,
                                            ALU.mult).then_inc(pair_back_in, 1)

            def add_sums(b, u, o, m):
                cols = slice(o * NQ, (o + 1) * NQ)
                powers = back[:, u, o:o + 1]
                if known(b, 2):
                    powers = pair_back[:, u, o:o + 1]
                    dve.wait_ge(pair_back_in, 2 * o + 2)
                dve.wait_ge(sums_filled, m + 1)
                dve.wait_ge(lora_drained, b * NO + (o + 1))
                nc.vector.scalar_tensor_tensor(out_sb[:, u, cols], sums[(m if isinstance(m, int) else o) % 2][:],
                                               powers, out_sb[:, u, cols], ALU.mult, ALU.add
                                               ).then_inc(sums_drained, 1)

            def batch(b, u, ahead):
                gates(b, u)
                if ahead:
                    find_x_top(b + 1)
                split_gated(b)
                if ahead:
                    split_x(b + 1)
                for o in range(2):
                    add_sums(b, u, o, b * NO + o)
                if ahead:
                    find_raw_top(b + 1)
                    split_x1(b + 1, 1 - u)
                for o in range(2, NO):
                    add_sums(b, u, o, b * NO + o)

            dve.wait_ge(ids_in, 32)
            dve.wait_ge(consts_made, 2)
            step(nc.vector.tensor_copy(lang_f[:], ids[:, 1, :]), bias_step, 1)
            nc.vector.tensor_scalar(tie_key[:], expert_no[:], -1.0 / 16, 0.5, ALU.mult, ALU.add)
            for e in range(E):
                nc.vector.tensor_scalar(bias[:, :, e], lang_f[:], expert_no[:, e:e + 1], LANG_BIAS,
                                        ALU.is_equal, ALU.mult)

            find_x_top(0)
            find_top(A)
            find_top(WR)
            split_x(0)
            scale_w(A)
            scale_w(WR)
            find_part(0, 0)
            split_pieces(0, ra_done)
            find_raw_top(0)
            find_part(0, 1)
            split_x1(0, 0)
            join_parts(0, 2)
            find_top(BT)
            scale_w(0)
            scale_w(BT)
            split_pieces(first_w[0], per_w)
            gates(0, 0)
            find_x_top(1)
            split_gated(0)
            split_x(1)
            split_pieces(first_b, b_done - first_b)
            find_raw_top(1)
            find_part(1, 0)
            split_x1(1, 1)
            powers_of_pair(0)
            find_part(1, 1)
            find_part(1, 2)
            gates(1, 1)
            find_part(1, 3)
            join_parts(1, 6)
            split_gated(1)
            scale_w(1)
            powers_of_pair(1)
            split_pieces(first_w[1], 4)
            for u in range(2):
                add_sums(u, u, 0, u)
            split_pieces(first_w[1] + 4, per_w - 4)
            for g in range(NG):
                find_part(2, g)
            join_parts(2, 10)
            scale_w(2)
            powers_of_pair(2)
            split_pieces(first_w[2], 4)
            for u in range(2):
                add_sums(u, u, 1, 2 + u)
            split_pieces(first_w[2] + 4, per_w - 4)
            find_x_top(2)
            find_part(3, 0)
            split_x(2)
            for g in range(1, NG):
                find_part(3, g)
            join_parts(3, 14)
            scale_w(3)
            powers_of_pair(3)
            split_pieces(first_w[3], 4)
            for u in range(2):
                add_sums(u, u, 2, 4 + u)
            split_pieces(first_w[3] + 4, per_w - 4)
            find_raw_top(2)
            split_x1(2, 0)
            for u in range(2):
                add_sums(u, u, 3, 6 + u)
            batch(2, 0, True)
            batch(3, 1, True)
            with dve.Fori(*LOOP) as pair:
                for u in range(2):
                    batch(pair * 2 + u, u, True)
            batch(B - 2, 0, True)
            batch(B - 1, 1, False)


def kernel(x, itok_B_0_15, itok_B_0_7, L0_cond_weights, L1_cond_W, L1_cond_Wr, L1_cond_A, L1_cond_B):
    import numpy as np
    import concourse.bacc as bacc
    from concourse.bass_utils import run_bass_kernel_spmd

    E, R, D = L1_cond_A.shape
    O = L1_cond_W.shape[0]
    arrays = {
        "x": x,
        "cond": itok_B_0_15,
        "lang": itok_B_0_7,
        "w0": L0_cond_weights,
        "wT": np.transpose(L1_cond_W),
        "wrT": np.transpose(L1_cond_Wr),
        "aT": np.transpose(np.reshape(L1_cond_A, (E * R, D))),
        "bT": np.reshape(np.transpose(L1_cond_B, (0, 2, 1)), (E * R, O)),
    }
    arrays = {name: np.ascontiguousarray(a) for name, a in arrays.items()}
    nc = bacc.Bacc("TRN2", target_bir_lowering=False, num_devices=1)
    args = [nc.dram_tensor(name, a.shape, mybir.dt.from_np(a.dtype), kind="ExternalInput").ap()
            for name, a in arrays.items()]
    args.append(nc.dram_tensor("out", x.shape, mybir.dt.float32, kind="ExternalOutput").ap())
    cond_resid_kernel(nc, *args)
    r = run_bass_kernel_spmd(nc, [arrays], core_ids=[0])
    return r.results[0]["out"]
```

```python
from contextlib import ExitStack

import concourse.bass as bass
from concourse import mybir

ALU = mybir.AluOpType
ACT = mybir.ActivationFunctionType
AX = mybir.AxisListType
F32 = mybir.dt.float32
F16 = mybir.dt.float16
I32 = mybir.dt.int32

P = 128
NQ = 512
TOP = 2.0 ** 14
LEAST = 2.0 ** -40
X1_DOWN = 1.0 / (2 * P * TOP)
EXPONENT = 0x7F800000
LANG_BIAS = 5.0
SCALING = 2.0
W_STEPS = 5
X_STEPS = 7
TURN_AT = 10
ROUTE_STEPS = 18


def cond_resid_kernel(nc, x, cond, lang, w0, wT, wrT, aT, bT, out):
    B, C, D = x.shape
    S = w0.shape[0]
    O = wT.shape[1]
    E = wrT.shape[1]
    ER = aT.shape[1]
    R = ER // E
    K = D // P
    NO = O // NQ
    RA = ER + E
    GROUP = NQ // P
    NG = K // GROUP
    HALF = 2
    assert C == P and ER == P and D == O and K == 4 * NO and B % 2 == 0 and B >= 6 and E == 8
    WR, A, BT = NO, NO + 1, NO + 2
    NW = NO + 3

    with ExitStack() as ctx:
        def sb(name, shape, dt):
            return ctx.enter_context(nc.sbuf_tensor(name, shape, dt))

        def sem(name):
            return ctx.enter_context(nc.semaphore(name))

        def bank(name):
            return ctx.enter_context(nc.psum_tensor(name, [P, NQ], F32))

        w_words = sb("w_words", [P, NO, K, NQ], F32)
        w_parts = w_words[:].bitcast(F16).rearrange("p o k (h n) -> p o k h n", h=2)
        ra_parts = sb("ra_parts", [P, K, 2, RA], F16)
        wr_words = sb("wr_words", [P, K, E], F32)
        b_parts = sb("b_parts", [P, NO, 2, NQ], F16)
        x_in = sb("x_in", [P, D], F32)
        wc_in = sb("wc_in", [P, P], F32)
        wc = sb("wc", [P, P], F32)
        x_parts = sb("x_parts", [P, 2, D], F16)
        wc_parts = sb("wc_parts", [P, 2, P], F16)
        spots = sb("spots", [P, 2, HALF, NQ], F32)
        x1_parts = sb("x1_parts", [P, 2, 2, K, P], F16)
        out_sb = sb("out_sb", [P, 2, D], F32)
        ident = sb("ident", [P, P], F32)
        ra = sb("ra", [P, RA], F32)
        chosen = sb("chosen", [P, E, R], F32)
        gated = sb("gated", [P, P], F32)
        gated_parts = sb("gated_parts", [P, 2, P], F16)
        ids = sb("ids", [P, 2, B], I32)
        lang_f = sb("lang_f", [P, B], F32)
        expert_no = sb("expert_no", [P, E], F32)
        tie_key = sb("tie_key", [P, E], F32)
        bias = sb("bias", [P, B, E], F32)
        w_max = sb("w_max", [P, NO, K // GROUP], F32)
        w_top = sb("w_top", [P, NW], F32)
        w_all = sb("w_all", [P, NW], F32)
        w_pow = sb("w_pow", [P, NW], F32)
        w_inv = sb("w_inv", [P, NW], F32)
        w_scale = sb("w_scale", [P, NW], F32)
        w_back = sb("w_back", [P, NW], F32)
        x_top = sb("x_top", [P, 2], F32)
        x_all = sb("x_all", [P, 2], F32)
        x_pow = sb("x_pow", [P, 2], F32)
        x_scale = sb("x_scale", [P, 2], F32)
        x_back = sb("x_back", [P, 2], F32)
        pair_back = sb("pair_back", [P, 2, NW], F32)
        back = sb("back", [P, 2, NW], F32)
        rt = sb("rt", [P, 6, E], F32)
        rs = sb("rs", [P, 8], F32)
        lora_back = sb("lora_back", [P, 2], F32)
        pool_scratch = sb("pool_scratch", [P, 1], F32)

        sums = [bank(f"sums{i}") for i in range(2)]
        lora = [bank(f"lora{i}") for i in range(2)]
        raw = [bank(f"raw{i}") for i in range(2)]
        ps_ra = bank("ps_ra")
        ps_g = bank("ps_g")

        LAST = NO - 1
        w_at = [w_words[:, min(o + 1, LAST)] for o in range(NO)]
        a_words = x1_parts[:, 1].rearrange("p h k n -> p (h k n)").bitcast(F32).rearrange("p (k n) -> p k n", n=ER)
        b_words = out_sb[:, 0, :].rearrange("p (o n) -> p o n", n=NQ)

        pieces = [(a_words, ra_parts[:, :, 0, 0:ER], ra_parts[:, :, 1, 0:ER], A, None),
                  (wr_words[:], ra_parts[:, :, 0, ER:RA], ra_parts[:, :, 1, ER:RA], WR, None)]
        ra_done = len(pieces)
        first_w = []
        early = [NG - 1] + list(range(NG - 1))
        split_order = [list(range(K // HALF)) for _ in range(NO)]
        split_order[LAST - 1] = [g * GROUP // HALF + i for g in early for i in range(GROUP // HALF)]
        for o in range(NO):
            first_w.append(len(pieces))
            for h in split_order[o]:
                ks = slice(h * HALF, (h + 1) * HALF)
                pieces.append((w_at[o][:, ks, :], w_parts[:, o, ks, 0, :], w_parts[:, o, ks, 1, :], o,
                               spots[:, h % 2] if o == LAST else None))
            if o == 0:
                first_b = len(pieces)
                pieces.append((b_words, b_parts[:, :, 0, :], b_parts[:, :, 1, :], BT, None))
                b_done = len(pieces)
        in_place = first_w[LAST]
        per_w = K // HALF
        small = [A, WR, BT]
        turn_of = {c: n for n, c in enumerate([A, WR, 0, BT, 1, 2, 3])}
        bounds = [A, WR, (0, 1), (0, 0), (0, 3), (1, 0), BT, (1, 1), (1, 2), (1, 3), (2, 0), (2, 1), (3, 0),
                  (3, 2)]
        bound_at = {what: n + 1 for n, what in enumerate(bounds)}

        def last_bound(o):
            return max(bound_at[what] for what in bounds if what not in small and what[0] == o)

        ids_in = sem("ids_in")
        a_in = sem("a_in")
        wr_in = sem("wr_in")
        b_in = sem("b_in")
        w_in = [[sem(f"w_in{o}_{g}") for g in range(NG)] for o in range(NO)]
        x_loaded = sem("x_loaded")
        matrix_loaded = sem("matrix_loaded")
        stored = [sem(f"stored{u}") for u in range(2)]
        zeroed = sem("zeroed")
        consts_made = sem("consts_made")
        diagonal_in = sem("diagonal_in")
        bias_step = sem("bias_step")
        bound_in = sem("bound_in")
        w_part_max = sem("w_part_max")
        top_found = sem("top_found")
        top_shared = sem("top_shared")
        w_step = sem("w_step")
        scaled_in = sem("scaled_in")
        w_high_in = sem("w_high_in")
        w_low_in = sem("w_low_in")
        x_top_found = sem("x_top_found")
        x_top_shared = sem("x_top_shared")
        x_step = sem("x_step")
        x_high_in = sem("x_high_in")
        x_low_in = sem("x_low_in")
        raw_filled = sem("raw_filled")
        x1_high_in = sem("x1_high_in")
        x1_low_in = sem("x1_low_in")
        back_in = sem("back_in")
        pair_back_in = sem("pair_back_in")
        ra_filled = sem("ra_filled")
        ra_low_out = sem("ra_low_out")
        route_step = sem("route_step")
        exp_in = sem("exp_in")
        gated_in = sem("gated_in")
        gated_turned = sem("gated_turned")
        gated_high_in = sem("gated_high_in")
        gated_low_in = sem("gated_low_in")
        lora_filled = sem("lora_filled")
        lora_drained = sem("lora_drained")
        sums_filled = sem("sums_filled")
        sums_drained = sem("sums_drained")

        block = ctx.enter_context(nc.Block())

        wT_dram = wT.rearrange("(k p) (o n) -> p o k n", p=P, n=NQ)
        x_halves = [slice(0, D // 2), slice(D // 2, D)]
        LOOP = (2, B // 2 - 1)

        def known(b, below):
            return isinstance(b, int) and b < below

        @block.sync
        def _(sp):
            def load_matrix(b):
                which = sp.value_load(ids[0:1, 0, bass.ds(b, 1)], min_val=0, max_val=S - 1)
                sp.dma_start(wc_in[:], w0[bass.ds(which, 1), :, :].rearrange("a c t -> (a c) t")
                             ).then_inc(matrix_loaded, 16)

            def load(b):
                sp.wait_ge(x_low_in, b * 3)
                sp.dma_start(x_in[:], x[bass.ds(b, 1), :, :].rearrange("a c t -> (a c) t")
                             ).then_inc(x_loaded, 16)
                load_matrix(b)

            def store(b, u, cols, m):
                sp.wait_ge(sums_drained, m)
                sp.dma_start(out[bass.ds(b, 1), :, cols].rearrange("a c t -> (a c) t"),
                             out_sb[:, u, cols]).then_inc(stored[u], 16)

            def load_w(o, gs=range(NG)):
                for n, g in enumerate(gs):
                    ks = slice(g * GROUP, (g + 1) * GROUP)
                    if o == LAST:
                        sp.wait_ge(w_low_in, first_w[o - 1] + (n + 1) * GROUP // HALF)
                    sp.dma_start(w_at[o][:, ks, :], wT_dram[:, o, ks, :]).then_inc(w_in[o][g], 16)

            front, back_cols = slice(0, LAST * NQ), slice(LAST * NQ, O)
            sp.dma_start(x_in[:], x[0]).then_inc(x_loaded, 16)
            sp.dma_start(ids[:, 0, :], cond.rearrange("(a b) -> a b", a=1).to_broadcast([P, B])).then_inc(ids_in, 16)
            sp.dma_start(ids[:, 1, :], lang.rearrange("(a b) -> a b", a=1).to_broadcast([P, B])).then_inc(ids_in, 16)
            sp.dma_start(a_words, aT.rearrange("(k p) n -> p k n", p=P)).then_inc(a_in, 16)
            sp.wait_ge(ids_in, 32)
            load_matrix(0)
            load_w(0, [1])
            sp.dma_start(wr_words[:], wrT.rearrange("(k p) n -> p k n", p=P)).then_inc(wr_in, 16)
            load_w(0, [0, 2, 3])
            load(1)
            sp.dma_start(out_sb[:, 0, :], bT).then_inc(b_in, 16)
            for o in range(1, NO):
                if o == LAST:
                    load(2)
                load_w(o, early if o == LAST else range(NG))
            load(3)
            for u in range(2):
                store(u, u, front, 2 * LAST)
            for u in range(2):
                store(u, u, back_cols, 2 * LAST + u + 1)

            def batch(b, u, loads):
                if loads:
                    load(b + 2)
                store(b, u, front, b * NO + LAST)
                store(b, u, back_cols, b * NO + NO)

            batch(2, 0, True)
            batch(3, 1, True)
            with sp.Fori(*LOOP) as pair:
                for u in range(2):
                    batch(pair * 2 + u, u, True)
            batch(B - 2, 0, False)
            batch(B - 1, 1, False)
            for u in range(2):
                sp.wait_ge(stored[u], 16 * B)

        @block.gpsimd
        def _(pool):
            def share(found, value, all_, top, shared):
                pool.wait_ge(found, value)
                nc.gpsimd.tensor_tensor(pool_scratch[:], expert_no[:, 0:1], expert_no[:, 0:1], ALU.add)
                nc.gpsimd.partition_all_reduce(all_, top, P, bass.bass_isa.ReduceOp.max).then_inc(shared, 1)


            def share_w(c, after=None):
                if after is not None:
                    pool.wait_ge(*after)
                col = slice(c, c + 1)
                found = (bound_in, bound_at[c]) if c in small else (top_found, c + 1)
                share(*found, w_all[:, col], w_top[:, col], top_shared)

            def share_x(b, after=None):
                if after is not None:
                    pool.wait_ge(*after)
                share(x_top_found, b + 1, x_all[:], x_top[:], x_top_shared)

            def add_diagonal(o):
                pool.wait_ge(w_in[o][o], 16)
                for g in range(GROUP):
                    spot = w_at[o][:, o * GROUP + g, g * P:(g + 1) * P]
                    ins = nc.gpsimd.tensor_tensor(spot, spot, ident[:], ALU.add)
                ins.then_inc(diagonal_in, 1)

            nc.gpsimd.memset(ident[:], 0.0).then_inc(zeroed, 1)
            nc.gpsimd.iota(expert_no[:], [[1, E]], base=0, channel_multiplier=0,
                           allow_small_or_imprecise_dtypes=True).then_inc(consts_made, 1)
            pool.wait_ge(zeroed, 1)
            nc.gpsimd.affine_select(out=ident[:], in_=ident[:], compare_op=ALU.not_equal, fill=1.0, base=0,
                                    pattern=[[-1, P]], channel_multiplier=1).then_inc(consts_made, 1)
            pool.wait_ge(consts_made, 2)
            share_x(0)
            share_w(A, (x_top_shared, 1))
            share_w(WR, (top_shared, 1))
            add_diagonal(0)
            share_w(0, (top_shared, 2))
            share_x(1, (top_shared, 3))
            add_diagonal(1)
            share_w(BT, (x_top_shared, 2))
            share_w(1, (top_shared, 4))
            add_diagonal(2)
            share_w(2, (top_shared, 5))
            share_x(2, (top_shared, 6))
            add_diagonal(3)
            share_w(3, (x_top_shared, 3))
            share_x(3, (top_shared, 7))
            for b in (2, 3):
                share_x(b + 2)
            with pool.Fori(*LOOP) as pair:
                for u in range(2):
                    share_x(pair * 2 + (u + 2))

        @block.tensor
        def _(pe):
            def layer0(b, gs=range(NG)):
                for g in gs:
                    if g in (gs[0], NG // 2):
                        pe.wait_ge(x_low_in, b * 3 + (2 + g // (NG // 2)))
                    if not known(b * NG + g, 2):
                        pe.wait_ge(x1_low_in, b * NG + (g - 1))
                    for j in range(GROUP):
                        k = g * GROUP + j
                        for left, right in ((0, 0), (0, 1), (1, 0)):
                            mm = nc.tensor.matmul(raw[g % 2][:, j * P:(j + 1) * P],
                                                  x_parts[:, left, k * P:(k + 1) * P], wc_parts[:, right, :],
                                                  start=(left + right == 0), stop=(left == 1))
                    mm.then_inc(raw_filled, 1)

            def ra_products(b, u):
                for k in range(K):
                    if known(b, 2) and k % GROUP == 0:
                        pe.wait_ge(x1_low_in, b * NG + k // GROUP + 1)
                    nc.tensor.matmul(ps_ra[:, 0:2 * RA], x1_parts[:, u, 0, k, :],
                                     ra_parts[:, k, :, :].rearrange("p h n -> p (h n)"), start=(k == 0), stop=False,
                                     skip_group_check=True)
                    mm = nc.tensor.matmul(ps_ra[:, 0:RA], x1_parts[:, u, 1, k, :], ra_parts[:, k, 0, :],
                                          start=False, stop=(k == K - 1), skip_group_check=True)
                return mm

            def products(bank, n, parts, u, ks=range(K), piece=None):
                for k in ks:
                    if piece is not None and k % HALF == 0:
                        pe.wait_ge(w_low_in, piece[k // HALF])
                    for left, right in ((0, 0), (0, 1), (1, 0)):
                        mm = nc.tensor.matmul(bank[:, 0:n], x1_parts[:, u, left, k, :], parts(k, right),
                                              start=(k == 0 and left + right == 0),
                                              stop=(k == K - 1 and left == 1))
                return mm

            def route(b, u):
                if known(b, 1):
                    pe.wait_ge(w_low_in, ra_done)
                else:
                    pe.wait_ge(route_step, (b - 1) * ROUTE_STEPS + 1)
                if not known(b, 2):
                    pe.wait_ge(x1_low_in, b * NG + NG)
                ra_products(b, u).then_inc(ra_filled, 1)

            def sums_block(u, o, m, between={}):
                piece = None
                if known(m, 2 * NO) and m == 2 * o:
                    piece = [first_w[o] + split_order[o].index(h) + 1 for h in range(per_w)]
                if not known(m, 2):
                    pe.wait_ge(sums_drained, m - 1)
                bank = sums[(m if isinstance(m, int) else o) % 2]
                parts = lambda k, part: w_parts[:, o, k, part, :]
                k = 0
                for at in sorted(between):
                    products(bank, NQ, parts, u, range(k, at), piece)
                    between[at]()
                    k = at
                products(bank, NQ, parts, u, range(k, K), piece).then_inc(sums_filled, 1)

            def turn_gated(b):
                pe.wait_ge(gated_in, b + 1)
                if not known(b, 1):
                    pe.wait_ge(gated_low_in, b)
                nc.tensor.transpose(ps_g[:, 0:P], gated[:], ident[:]).then_inc(gated_turned, 1)

            def lora_product(b, js=range(NO)):
                pe.wait_ge(gated_high_in, b + 1)
                pe.wait_ge(gated_low_in, b + 1)
                if known(b, 1):
                    pe.wait_ge(w_low_in, b_done)
                for j in js:
                    if not known(b * NO + j, 2):
                        pe.wait_ge(lora_drained, b * NO + (j - 1))
                    for left, right in ((0, 0), (0, 1), (1, 0)):
                        mm = nc.tensor.matmul(lora[j % 2][:], gated_parts[:, left, :], b_parts[:, j, right, :],
                                              start=(left + right == 0), stop=(left == 1))
                    mm.then_inc(lora_filled, 1)

            def batch(b, u, ahead):
                route(b, u)
                sums_block(u, 0, b * NO, {TURN_AT: lambda: turn_gated(b)})
                for h in range(2):
                    lora_product(b, range(2 * h, 2 * h + 2))
                    if ahead:
                        layer0(b + 1, range(2 * h, 2 * h + 2))
                for o in range(1, NO):
                    sums_block(u, o, b * NO + o)

            layer0(0)
            route(0, 0)
            sums_block(0, 0, 0, {12: lambda: layer0(1, range(0, 2)), 14: lambda: layer0(1, range(2, 4))})
            route(1, 1)
            sums_block(1, 0, 1, {6: lambda: turn_gated(0), 9: lambda: lora_product(0)})
            turn_gated(1)
            for o in range(1, NO):
                sums_block(0, o, 2 * o, {4: lambda: lora_product(1)} if o == 1 else {})
                if o == LAST:
                    sums_block(1, o, 2 * o + 1, {4: lambda: layer0(2, range(0, 2)), 9: lambda: layer0(2, range(2, 4))})
                else:
                    sums_block(1, o, 2 * o + 1)
            batch(2, 0, True)
            batch(3, 1, True)
            with pe.Fori(*LOOP) as pair:
                for u in range(2):
                    batch(pair * 2 + u, u, True)
            batch(B - 2, 0, True)
            batch(B - 1, 1, False)

        @block.scalar
        def _(act):
            def split_piece(n):
                words, high, low, c, spot = pieces[n]
                scale = w_scale[:, c:c + 1]
                act.wait_ge(w_step, W_STEPS * turn_of[c] + W_STEPS)
                if spot is None:
                    nc.scalar.activation(high, words, ACT.Copy, scale=scale).then_inc(w_high_in, 1)
                    return
                act.wait_ge(w_low_in, n - 1)
                if n == in_place:
                    act.wait_ge(bound_in, len(bounds))
                nc.scalar.activation(spot, words, ACT.Copy, scale=scale).then_inc(scaled_in, 1)
                act.wait_ge(scaled_in, n - in_place + 1)
                nc.scalar.activation(high, spot, ACT.Copy).then_inc(w_high_in, 1)

            def bound(what):
                if what in small:
                    arrived, words = {A: (a_in, a_words), WR: (wr_in, wr_words[:]), BT: (b_in, b_words)}[what]
                    act.wait_ge(arrived, 16)
                    into = w_top[:, what:what + 1]
                else:
                    o, g = what
                    act.wait_ge(w_in[o][g], 16)
                    if o == g:
                        act.wait_ge(diagonal_in, o + 1)
                    words = w_at[o][:, g * GROUP:(g + 1) * GROUP, :]
                    into = w_max[:, o, g:g + 1]
                if bound_at[what] > 1:
                    act.wait_ge(bound_in, bound_at[what] - 1)
                rows, n = words.shape[1:]
                unused = spots[:].rearrange("p a h n -> p (a h n)")[:, 0:rows * n]
                nc.scalar.activation(unused.rearrange("p (k n) -> p k n", n=n), words, ACT.Abs,
                                     accum_out=into).then_inc(bound_in, 1)

            def split_x(b):
                act.wait_ge(x_step, b * X_STEPS + 5)
                if not known(b, 1):
                    act.wait_ge(raw_filled, b * NG)
                for half in x_halves:
                    nc.scalar.activation(x_parts[:, 0, half], x_in[:, half], ACT.Copy, scale=x_scale[:, 0:1]
                                         ).then_inc(x_high_in, 1)

            def split_x1(b, u, gs=range(NG)):
                if known(b, 2):
                    if b == 1:
                        act.wait_ge(w_low_in, ra_done)
                else:
                    act.wait_ge(sums_filled, 2 * LAST + 1 if known(b, 3) else (b - 1) * NO)
                for g in gs:
                    act.wait_ge(raw_filled, b * NG + (g + 1))
                    nc.scalar.activation(x1_parts[:, u, 0, g * GROUP:(g + 1) * GROUP, :].rearrange("p k n -> p (k n)"),
                                         raw[g % 2][:], ACT.Copy, scale=X1_DOWN).then_inc(x1_high_in, 1)

            def copy_ra(b):
                act.wait_ge(ra_filled, b + 1)
                if not known(b, 1):
                    act.wait_ge(route_step, b * ROUTE_STEPS)
                nc.scalar.activation(ra[:], ps_ra[:, RA:2 * RA], ACT.Copy).then_inc(ra_low_out, 1)

            def exponentials(b):
                act.wait_ge(route_step, b * ROUTE_STEPS + 7)
                nc.scalar.activation(rt[:, 3, :], rt[:, 2, :], ACT.Exp).then_inc(exp_in, 1)

            def split_gated(b):
                act.wait_ge(gated_turned, b + 1)
                if known(b, 2) and b == 1:
                    act.wait_ge(lora_filled, NO)
                nc.scalar.activation(gated_parts[:, 0, :], ps_g[:, 0:P], ACT.Copy).then_inc(gated_high_in, 1)

            def copy_lora(b, u, js=range(NO)):
                act.wait_ge(route_step, b * ROUTE_STEPS + ROUTE_STEPS)
                if known(b, 2):
                    act.wait_ge(w_low_in, b_done)
                else:
                    act.wait_ge(stored[u], b * 16 - 16 * u)
                for j in js:
                    act.wait_ge(lora_filled, b * NO + (j + 1))
                    nc.scalar.activation(out_sb[:, u, j * NQ:(j + 1) * NQ], lora[j % 2][:], ACT.Copy,
                                         scale=lora_back[:, u:u + 1]).then_inc(lora_drained, 1)

            def split_pieces(first, count):
                for n in range(first, first + count):
                    split_piece(n)

            def batch(b, u, ahead):
                copy_ra(b)
                exponentials(b)
                split_gated(b)
                if ahead:
                    split_x(b + 1)
                for h in range(2):
                    copy_lora(b, u, range(2 * h, 2 * h + 2))
                    if ahead:
                        split_x1(b + 1, 1 - u, range(2 * h, 2 * h + 2))

            bound(A)
            split_x(0)
            bound(WR)
            split_pieces(0, 1)
            split_x1(0, 0, range(0, 2))
            bound((0, 1))
            split_x1(0, 0, range(2, 4))
            split_pieces(1, 1)
            bound((0, 0))
            bound((0, 3))
            split_pieces(first_w[0], 6)
            copy_ra(0)
            split_pieces(first_w[0] + 6, 2)
            split_x(1)
            bound((1, 0))
            bound(BT)
            split_x1(1, 1, range(0, 2))
            bound((1, 1))
            split_x1(1, 1, range(2, 4))
            bound((1, 2))
            exponentials(0)
            bound((1, 3))
            split_pieces(first_b, 1)
            copy_ra(1)
            split_gated(0)
            split_pieces(first_w[1], 1)
            copy_lora(0, 0, range(0, 2))
            exponentials(1)
            copy_lora(0, 0, range(2, 4))
            split_pieces(first_w[1] + 1, 3)
            split_gated(1)
            split_pieces(first_w[1] + 4, 3)
            copy_lora(1, 1)
            split_pieces(first_w[1] + 7, 1)
            for g in range(2):
                bound((2, g))
            split_pieces(first_w[2], per_w)
            bound((3, 0))
            bound((3, 2))
            split_pieces(first_w[3], per_w)
            split_x(2)
            split_x1(2, 0)
            batch(2, 0, True)
            batch(3, 1, True)
            with act.Fori(*LOOP) as pair:
                for u in range(2):
                    batch(pair * 2 + u, u, True)
            batch(B - 2, 0, True)
            batch(B - 1, 1, False)

        @block.vector
        def _(dve):
            def step(ins, which, value):
                ins.then_inc(which, 1)
                dve.wait_ge(which, value)

            def power_and_inverse(which, s, all_, pow_, inv):
                step(nc.vector.tensor_scalar(all_, all_, LEAST, None, ALU.max), which, s + 1)
                step(nc.vector.tensor_scalar(pow_.bitcast(I32), all_.bitcast(I32), EXPONENT, None,
                                             ALU.bitwise_and), which, s + 2)
                step(nc.vector.reciprocal(inv, pow_), which, s + 3)

            def find_part(o, g):
                dve.wait_ge(w_in[o][g], 16)
                if g == o:
                    dve.wait_ge(diagonal_in, o + 1)
                nc.vector.tensor_reduce(w_max[:, o, g:g + 1], w_at[o][:, g * GROUP:(g + 1) * GROUP, :],
                                        AX.XY, ALU.max, apply_absolute_value=True).then_inc(w_part_max, 1)

            def join_parts(o, found):
                dve.wait_ge(w_part_max, found)
                dve.wait_ge(bound_in, last_bound(o))
                nc.vector.tensor_reduce(w_top[:, o:o + 1], w_max[:, o, :], AX.X, ALU.max).then_inc(top_found, 1)

            def scale_w(c):
                col = slice(c, c + 1)
                s = turn_of[c] * W_STEPS
                dve.wait_ge(top_shared, turn_of[c] + 1)
                power_and_inverse(w_step, s, w_all[:, col], w_pow[:, col], w_inv[:, col])
                nc.vector.tensor_scalar(w_back[:, col], w_pow[:, col], 1.0 / TOP, None, ALU.mult).then_inc(w_step, 1)
                nc.vector.tensor_scalar(w_scale[:, col], w_inv[:, col], TOP, None, ALU.mult).then_inc(w_step, 1)

            def split_pieces(first, count):
                for n in range(first, first + count):
                    words, high, low, c, spot = pieces[n]
                    dve.wait_ge(w_high_in, n + 1)
                    if spot is None:
                        nc.vector.scalar_tensor_tensor(low, words, w_scale[:, c:c + 1], high, ALU.mult, ALU.subtract
                                                       ).then_inc(w_low_in, 1)
                    else:
                        nc.vector.tensor_tensor(low, spot, high, ALU.subtract).then_inc(w_low_in, 1)

            def find_x_top(b):
                dve.wait_ge(x_loaded, b * 16 + 16)
                nc.vector.tensor_reduce(x_top[:, 0:1], x_in[:], AX.X, ALU.max, apply_absolute_value=True)
                dve.wait_ge(matrix_loaded, b * 16 + 16)
                if not known(b, 1):
                    dve.wait_ge(x_low_in, b * 3)
                s = b * X_STEPS
                nc.vector.tensor_tensor(wc[:], wc_in[:], ident[:], ALU.add).then_inc(x_step, 1)
                dve.wait_ge(x_step, s + 1)
                nc.vector.tensor_reduce(x_top[:, 1:2], wc[:], AX.X, ALU.max, apply_absolute_value=True
                                        ).then_inc(x_top_found, 1)

            def scale_x(b, u):
                s = b * X_STEPS
                dve.wait_ge(x_top_shared, b + 1)
                power_and_inverse(x_step, s + 1, x_all[:], x_pow[:], x_scale[:])
                step(nc.vector.tensor_scalar(x_scale[:], x_scale[:], TOP, None, ALU.mult), x_step, s + 5)
                powers = x_back[:, u:u + 1]
                nc.vector.tensor_scalar(powers, x_pow[:, 0:1], x_pow[:, 1:2], 1.0 / (TOP * TOP * X1_DOWN),
                                        ALU.mult, ALU.mult).then_inc(x_step, 1)
                if not known(b, 1):
                    dve.wait_ge(raw_filled, b * NG)
                step(nc.vector.tensor_scalar(wc_parts[:, 0, :], wc[:], x_scale[:, 1:2], None, ALU.mult),
                     x_step, s + 7)
                if not known(b, 2):
                    nc.vector.tensor_scalar(back[:, u, :], w_back[:], powers, None, ALU.mult).then_inc(back_in, 1)
                nc.vector.scalar_tensor_tensor(wc_parts[:, 1, :], wc[:], x_scale[:, 1:2], wc_parts[:, 0, :],
                                               ALU.mult, ALU.subtract).then_inc(x_low_in, 1)

            def split_x(b):
                for n, half in enumerate(x_halves):
                    dve.wait_ge(x_high_in, b * 2 + (n + 1))
                    nc.vector.scalar_tensor_tensor(x_parts[:, 1, half], x_in[:, half], x_scale[:, 0:1],
                                                   x_parts[:, 0, half], ALU.mult, ALU.subtract).then_inc(x_low_in, 1)

            def split_x1(b, u, gs=range(NG)):
                for g in gs:
                    dve.wait_ge(x1_high_in, b * NG + (g + 1))
                    high, low = (x1_parts[:, u, h, g * GROUP:(g + 1) * GROUP, :].rearrange("p k n -> p (k n)")
                                 for h in range(2))
                    nc.vector.scalar_tensor_tensor(low, raw[g % 2][:], X1_DOWN, high, ALU.mult, ALU.subtract
                                                   ).then_inc(x1_low_in, 1)

            def gates(b, u):
                dve.wait_ge(ra_filled, b + 1)
                dve.wait_ge(ra_low_out, b + 1)
                if known(b, 2):
                    powers = pair_back
                    dve.wait_ge(pair_back_in, 2)
                else:
                    powers = back
                    dve.wait_ge(back_in, b - 1)
                r = b * ROUTE_STEPS
                lg, best, less, ex, key, best_key = (rt[:, i, :] for i in range(6))
                total, inv_total, factor, weight, row_top, row_pow, row_inv, row_scale = (
                    rs[:, i:i + 1] for i in range(8))
                step(nc.vector.tensor_tensor(ra[:], ps_ra[:, 0:RA], ra[:], ALU.add), route_step, r + 1)
                step(nc.vector.scalar_tensor_tensor(lg, ra[:, ER:RA], powers[:, u, WR:WR + 1],
                                                    bias[:, bass.ds(b, 1), :].rearrange("p a e -> p (a e)"),
                                                    ALU.mult, ALU.add), route_step, r + 2)
                nc.vector.tensor_scalar(factor, powers[:, u, A:A + 1], SCALING / TOP, None, ALU.mult
                                        ).then_inc(route_step, 1)
                step(nc.vector.max(best, lg), route_step, r + 4)
                step(nc.vector.scalar_tensor_tensor(key, lg, best[:, 1:2], tie_key[:], ALU.is_equal, ALU.mult),
                     route_step, r + 5)
                step(nc.vector.scalar_tensor_tensor(key, lg, best[:, 1:2], key, ALU.is_gt, ALU.add),
                     route_step, r + 6)
                nc.vector.tensor_scalar(less, lg, best[:, 0:1], None, ALU.subtract).then_inc(route_step, 1)
                step(nc.vector.max(best_key, key), route_step, r + 8)
                dve.wait_ge(exp_in, b + 1)
                step(nc.vector.scalar_tensor_tensor(key, key, best_key[:, 1:2], ex, ALU.is_ge, ALU.mult,
                                                    accum_out=total), route_step, r + 9)
                step(nc.vector.reciprocal(inv_total, total), route_step, r + 10)
                step(nc.vector.tensor_scalar(weight, inv_total, factor, None, ALU.mult), route_step, r + 11)
                step(nc.vector.tensor_tensor(chosen[:], ra[:, 0:ER].rearrange("p (e r) -> p e r", e=E),
                                             key.rearrange("p (e a) -> p e a", a=1).to_broadcast([P, E, R]),
                                             ALU.mult), route_step, r + 12)
                step(nc.vector.tensor_reduce(row_top, chosen[:], AX.XY, ALU.max, apply_absolute_value=True),
                     route_step, r + 13)
                power_and_inverse(route_step, r + 13, row_top, row_pow, row_inv)
                nc.vector.tensor_scalar(lora_back[:, u:u + 1], row_pow, weight, w_back[:, BT:BT + 1],
                                        ALU.mult, ALU.mult).then_inc(route_step, 1)
                step(nc.vector.tensor_scalar(row_scale, row_inv, TOP, None, ALU.mult), route_step, r + 18)
                if not known(b, 1):
                    dve.wait_ge(gated_turned, b)
                nc.vector.tensor_scalar(gated[:], chosen[:].rearrange("p e r -> p (e r)"), row_scale, None, ALU.mult
                                        ).then_inc(gated_in, 1)

            def split_gated(b):
                dve.wait_ge(gated_high_in, b + 1)
                if not known(b, 1):
                    dve.wait_ge(lora_filled, b * NO)
                nc.vector.tensor_tensor(gated_parts[:, 1, :], ps_g[:, 0:P], gated_parts[:, 0, :], ALU.subtract
                                        ).then_inc(gated_low_in, 1)

            def powers_of_pair(cols):
                for u in range(2):
                    nc.vector.tensor_scalar(pair_back[:, u, cols], w_back[:, cols], x_back[:, u:u + 1], None,
                                            ALU.mult).then_inc(pair_back_in, 1)

            def add_sums(b, u, o, m):
                cols = slice(o * NQ, (o + 1) * NQ)
                powers = back[:, u, o:o + 1]
                if known(b, 2):
                    powers = pair_back[:, u, o:o + 1]
                    dve.wait_ge(pair_back_in, 2 * o + 4)
                dve.wait_ge(sums_filled, m + 1)
                dve.wait_ge(lora_drained, b * NO + (o + 1))
                nc.vector.scalar_tensor_tensor(out_sb[:, u, cols], sums[(m if isinstance(m, int) else o) % 2][:],
                                               powers, out_sb[:, u, cols], ALU.mult, ALU.add
                                               ).then_inc(sums_drained, 1)

            def batch(b, u, ahead, top_ahead):
                gates(b, u)
                if ahead:
                    scale_x(b + 1, 1 - u)
                split_gated(b)
                if ahead:
                    split_x(b + 1)
                add_sums(b, u, 0, b * NO)
                if ahead:
                    split_x1(b + 1, 1 - u)
                for o in range(1, NO):
                    add_sums(b, u, o, b * NO + o)
                if top_ahead:
                    find_x_top(b + 2)

            dve.wait_ge(consts_made, 2)
            find_x_top(0)
            dve.wait_ge(ids_in, 32)
            step(nc.vector.tensor_copy(lang_f[:], ids[:, 1, :]), bias_step, 1)
            nc.vector.tensor_scalar(tie_key[:], expert_no[:], -1.0 / 16, 0.5, ALU.mult, ALU.add)
            for e in range(E):
                nc.vector.tensor_scalar(bias[:, :, e], lang_f[:], expert_no[:, e:e + 1], LANG_BIAS,
                                        ALU.is_equal, ALU.mult)

            scale_x(0, 0)
            scale_w(A)
            split_x(0)
            scale_w(WR)
            split_x1(0, 0, range(0, 2))
            split_pieces(0, 1)
            split_x1(0, 0, range(2, 4))
            find_part(0, 2)
            split_pieces(1, 1)
            join_parts(0, 1)
            scale_w(0)
            split_pieces(first_w[0], 2)
            find_x_top(1)
            split_pieces(first_w[0] + 2, 2)
            scale_x(1, 1)
            split_pieces(first_w[0] + 4, 2)
            split_x(1)
            split_pieces(first_w[0] + 6, 2)
            split_x1(1, 1, range(0, 2))
            scale_w(BT)
            split_x1(1, 1, range(2, 4))
            dve.wait_ge(w_step, 4 * W_STEPS)
            powers_of_pair(slice(WR, A + 1))
            powers_of_pair(slice(0, 1))
            gates(0, 0)
            join_parts(1, 1)
            split_pieces(first_b, 1)
            scale_w(1)
            dve.wait_ge(w_step, 5 * W_STEPS)
            powers_of_pair(slice(1, 2))
            split_gated(0)
            gates(1, 1)
            split_pieces(first_w[1], 1)
            add_sums(0, 0, 0, 0)
            split_pieces(first_w[1] + 1, 3)
            split_gated(1)
            split_pieces(first_w[1] + 4, 3)
            find_part(2, 3)
            split_pieces(first_w[1] + 7, 1)
            add_sums(1, 1, 0, 1)
            find_part(2, 2)
            join_parts(2, 3)
            scale_w(2)
            dve.wait_ge(w_step, 6 * W_STEPS)
            powers_of_pair(slice(2, 3))
            add_sums(0, 0, 1, 2)
            split_pieces(first_w[2], per_w)
            find_x_top(2)
            add_sums(1, 1, 1, 3)
            find_part(3, 1)
            find_part(3, 3)
            join_parts(3, 5)
            scale_w(3)
            dve.wait_ge(w_step, 7 * W_STEPS)
            powers_of_pair(slice(3, 4))
            split_pieces(first_w[3], 1)
            scale_x(2, 0)
            split_pieces(first_w[3] + 1, 1)
            add_sums(0, 0, 2, 4)
            split_pieces(first_w[3] + 2, 4)
            add_sums(1, 1, 2, 5)
            split_pieces(first_w[3] + 6, 2)
            split_x(2)
            add_sums(0, 0, 3, 6)
            split_x1(2, 0)
            find_x_top(3)
            add_sums(1, 1, 3, 7)
            batch(2, 0, True, True)
            batch(3, 1, True, True)
            with dve.Fori(*LOOP) as pair:
                for u in range(2):
                    batch(pair * 2 + u, u, True, True)
            batch(B - 2, 0, True, False)
            batch(B - 1, 1, False, False)


def kernel(x, itok_B_0_15, itok_B_0_7, L0_cond_weights, L1_cond_W, L1_cond_Wr, L1_cond_A, L1_cond_B):
    import numpy as np
    import concourse.bacc as bacc
    from concourse.bass_utils import run_bass_kernel_spmd

    E, R, D = L1_cond_A.shape
    O = L1_cond_W.shape[0]
    arrays = {
        "x": x,
        "cond": itok_B_0_15,
        "lang": itok_B_0_7,
        "w0": L0_cond_weights,
        "wT": np.transpose(L1_cond_W),
        "wrT": np.transpose(L1_cond_Wr),
        "aT": np.transpose(np.reshape(L1_cond_A, (E * R, D))),
        "bT": np.reshape(np.transpose(L1_cond_B, (0, 2, 1)), (E * R, O)),
    }
    arrays = {name: np.ascontiguousarray(a) for name, a in arrays.items()}
    nc = bacc.Bacc("TRN2", target_bir_lowering=False, num_devices=1)
    args = [nc.dram_tensor(name, a.shape, mybir.dt.from_np(a.dtype), kind="ExternalInput").ap()
            for name, a in arrays.items()]
    args.append(nc.dram_tensor("out", x.shape, mybir.dt.float32, kind="ExternalOutput").ap())
    cond_resid_kernel(nc, *args)
    r = run_bass_kernel_spmd(nc, [arrays], core_ids=[0])
    return r.results[0]["out"]
```
